# Optimizing a Trainium2 kernel written in Bass

```python
import numpy as np
import jax
import jax.numpy as jnp

def _softmax(x, axis=-1):
    return jax.nn.softmax(x, axis=axis)

def _gelu(x):
    return jax.nn.gelu(x, approximate=True)

def _silu(x):
    return jax.nn.silu(x)

def _sigmoid(x):
    return jax.nn.sigmoid(x)

def _layernorm(x, axis=-1, eps=1e-05):
    m = jnp.mean(x, axis=axis, keepdims=True)
    v = jnp.var(x, axis=axis, keepdims=True)
    return (x - m) / jnp.sqrt(v + eps)

def _scatter_add(tgt, idx, src, axis=0):
    return tgt.at[idx].add(src)

def _segment_sum(src, seg, n):
    return jax.ops.segment_sum(src, seg, n)
kernel_name = 'mk_gnn_resnorm_d2_gnn_r8_ee3a6b'

def setup_inputs(seed: int=0):
    np.random.seed(seed)
    _w = jnp.asarray

    def _rec_inputs():
        import jax
        import jax.numpy as jnp
        _gk = jax.random.key(seed)
        x = -0.0002117 + 1 * jax.random.normal(jax.random.fold_in(_gk, 1), (6250, 512), jnp.float32)
        src = jax.random.randint(jax.random.fold_in(_gk, 2), (100000,), 0, 6250, jnp.int32)
        dst = jax.random.randint(jax.random.fold_in(_gk, 3), (100000,), 0, 6250, jnp.int32)
        _o = jnp.argsort(dst, stable=True)
        src = src[_o]
        dst = dst[_o]
        return (x, src, dst)
    x, src, dst = _rec_inputs()

    def _L0_gnn_setup():
        import jax, jax.numpy as jnp
        import numpy as np
        N_NODES = 6250
        N_EDGES = 18750
        D_IN = 512
        D_OUT = 512
        LN_EPS = 1e-05
        key = jax.random.key(seed)
        k_x, k_e, k_ws, k_wn = jax.random.split(key, 4)
        x = jax.random.normal(k_x, (N_NODES, D_IN), dtype=jnp.float32)
        edge_index = jax.random.randint(k_e, (2, N_EDGES), 0, N_NODES, dtype=jnp.int64)
        scale = 1.0 / np.sqrt(D_IN)
        w_self = jax.random.normal(k_ws, (D_OUT, D_IN), dtype=jnp.float32) * scale
        w_neigh = jax.random.normal(k_wn, (D_OUT, D_IN), dtype=jnp.float32) * scale
        bias = jnp.zeros((D_OUT,), dtype=jnp.float32)
        gamma = jnp.ones((D_OUT,), dtype=jnp.float32)
        beta = jnp.zeros((D_OUT,), dtype=jnp.float32)
        return {'x': x, 'edge_index': edge_index, 'w_self': w_self, 'w_neigh': w_neigh, 'bias': bias, 'gamma': gamma, 'beta': beta}
    _L0_gnn_all = _L0_gnn_setup()
    _L0_gnn_in = {k: v for k, v in _L0_gnn_all.items() if k in ('w_self', 'w_neigh', 'bias', 'gamma', 'beta')}
    del _L0_gnn_all

    def _L1_gnn_setup():
        import jax, jax.numpy as jnp
        import numpy as np
        N_NODES = 6250
        N_EDGES = 187500
        D = 512
        LN_EPS = 1e-05

        def _layer_norm(x, gamma, beta):
            mu = jnp.mean(x, axis=-1, keepdims=True)
            var = jnp.mean(jnp.square(x - mu), axis=-1, keepdims=True)
            return (x - mu) * jax.lax.rsqrt(var + LN_EPS) * gamma + beta
        key = jax.random.key(seed)
        ks = jax.random.split(key, 8)
        scale = 1.0 / np.sqrt(D)
        return {'node_feature': jax.random.normal(ks[0], (N_NODES, D), dtype=jnp.float32), 'edge_index': jax.random.randint(ks[1], (2, N_EDGES), 0, N_NODES, dtype=jnp.int32), 'W_l': jax.random.uniform(ks[2], (D, D), jnp.float32, -scale, scale), 'b_l': jnp.zeros((D,), jnp.float32), 'W_r': jax.random.uniform(ks[3], (D, D), jnp.float32, -scale, scale), 'gamma': jnp.ones((D,), jnp.float32), 'beta': jnp.zeros((D,), jnp.float32)}
    _L1_gnn_all = _L1_gnn_setup()
    _L1_gnn_in = {k: v for k, v in _L1_gnn_all.items() if k in ('W_l', 'b_l', 'W_r', 'gamma', 'beta')}
    del _L1_gnn_all
    return {'x': x, 'src': src, 'dst': dst, 'L0_gnn_w_self': _L0_gnn_in['w_self'], 'L0_gnn_w_neigh': _L0_gnn_in['w_neigh'], 'L0_gnn_bias': _L0_gnn_in['bias'], 'L0_gnn_gamma': _L0_gnn_in['gamma'], 'L0_gnn_beta': _L0_gnn_in['beta'], 'L1_gnn_W_l': _L1_gnn_in['W_l'], 'L1_gnn_b_l': _L1_gnn_in['b_l'], 'L1_gnn_W_r': _L1_gnn_in['W_r'], 'L1_gnn_gamma': _L1_gnn_in['gamma'], 'L1_gnn_beta': _L1_gnn_in['beta']}

def reference(x, src, dst, L0_gnn_w_self, L0_gnn_w_neigh, L0_gnn_bias, L0_gnn_gamma, L0_gnn_beta, L1_gnn_W_l, L1_gnn_b_l, L1_gnn_W_r, L1_gnn_gamma, L1_gnn_beta):
    import jax
    import jax.numpy as jnp

    def _L0_gnn_ref(x, edge_index, w_self, w_neigh, bias, gamma, beta):
        import jax, jax.numpy as jnp
        import numpy as np
        N_NODES = 6250
        N_EDGES = 18750
        D_IN = 512
        D_OUT = 512
        LN_EPS = 1e-05
        n = x.shape[0]
        s, d = (edge_index[0], edge_index[1])
        agg = jax.ops.segment_sum(x[s], d, num_segments=n)
        cnt = jax.ops.segment_sum(jnp.ones(s.shape[0], x.dtype), d, num_segments=n)
        agg = agg / jnp.maximum(cnt, 1.0)[:, None]
        h = x @ w_self.T + agg @ w_neigh.T + bias
        mu = jnp.mean(h, axis=-1, keepdims=True)
        var = jnp.mean(jnp.square(h - mu), axis=-1, keepdims=True)
        hn = (h - mu) * jax.lax.rsqrt(var + LN_EPS) * gamma + beta
        return jax.nn.relu(hn)

    def _L1_gnn_ref(node_feature, edge_index, W_l, b_l, W_r, gamma, beta):
        import jax, jax.numpy as jnp
        import numpy as np
        N_NODES = 6250
        N_EDGES = 187500
        D = 512
        LN_EPS = 1e-05

        def _layer_norm(x, gamma, beta):
            mu = jnp.mean(x, axis=-1, keepdims=True)
            var = jnp.mean(jnp.square(x - mu), axis=-1, keepdims=True)
            return (x - mu) * jax.lax.rsqrt(var + LN_EPS) * gamma + beta
        n = node_feature.shape[0]
        residual = node_feature
        h = _layer_norm(node_feature, gamma, beta)
        src, dst = (edge_index[0], edge_index[1])
        summed = jax.ops.segment_sum(h[src], dst, num_segments=n)
        cnt = jax.ops.segment_sum(jnp.ones((src.shape[0],), h.dtype), dst, num_segments=n)
        mean = summed / jnp.maximum(cnt, 1.0)[:, None]
        out = mean @ W_l.T + b_l + h @ W_r.T
        out = jax.nn.relu(out)
        return out + residual
    edge_index = jnp.stack([src, dst])
    x = _layernorm(x + _L0_gnn_ref(x, edge_index, L0_gnn_w_self, L0_gnn_w_neigh, L0_gnn_bias, L0_gnn_gamma, L0_gnn_beta), axis=-1)
    x = _layernorm(x + _L1_gnn_ref(x, edge_index, L1_gnn_W_l, L1_gnn_b_l, L1_gnn_W_r, L1_gnn_gamma, L1_gnn_beta), axis=-1)
    return x

_drawn_inputs = setup_inputs


def setup_inputs(seed=0):
    import zlib

    import numpy as np

    out = dict(_drawn_inputs(seed))
    spreads = {'L0_gnn_bias': (0.0, 0.1),
     'L0_gnn_gamma': (1.0, 0.2),
     'L0_gnn_beta': (0.0, 0.1),
     'L1_gnn_b_l': (0.0, 0.1),
     'L1_gnn_gamma': (1.0, 0.2),
     'L1_gnn_beta': (0.0, 0.289)}
    factors = {}
    for name, (base, spread) in spreads.items():
        noise = np.random.default_rng([zlib.crc32(name.encode()), seed]).standard_normal(out[name].shape)
        drawn = base * np.exp(spread * noise) if base else spread * noise
        out[name] = jnp.asarray(drawn.astype(out[name].dtype))
    for name, factor in factors.items():
        out[name] = (out[name] * factor).astype(out[name].dtype)
    return out
```

```python
from contextlib import ExitStack

import concourse.bass as bass
from concourse import mybir

F32 = mybir.dt.float32
I32 = mybir.dt.int32
ALU = mybir.AluOpType
ACT = mybir.ActivationFunctionType
AX_X = mybir.AxisListType.X

N, E, D = 6250, 100000, 512
EPS = 1e-5
PN = 125
NT = N // PN
CH = 17
CAP = CH * 128
KC = D // 128
ER = E // 125
GT = E // 125
HI = 64
FAR = 1.0e6
DX = D + 2

C_ID, C_IOTA, C_THR, C_TRI, C_ONE = 0, 128, 256, 384, 512
C_THRC, C_BASE, C_DUMP = 640, 641, 641 + NT
C_EPS = C_DUMP + 1
C_ALL = C_EPS + 1


def constants(np):
    c = np.zeros((128, C_ALL), np.float32)
    p = np.arange(128)
    c[:, C_ID:C_ID + 128] = np.eye(128)
    c[:, C_IOTA:C_IOTA + 128] = p
    thr = np.where(p < HI, PN * p, PN * (p - HI + 1))
    c[:, C_THR:C_THR + 128] = thr
    c[:, C_TRI:C_TRI + 128] = p[None, :] < p[:, None]
    c[:, C_ONE:C_ONE + 128] = 1.0
    c[:, C_THRC] = thr
    c[:, C_BASE:C_BASE + NT] = PN * np.arange(NT)
    c[:, C_DUMP] = N + p
    c[:, C_EPS] = EPS
    return c


def wait(eng, sem, value):
    if not isinstance(value, int) or value > 0:
        eng.wait_ge(sem, value)


def hold(eng, sem, value, tick):
    wait(eng, sem, value)
    if not isinstance(value, int):
        eng.sem_inc(tick, 1)


def over_tiles(eng, body):
    body(0, 0, 0)
    body(1, 1, 0)
    with eng.Fori(1, NT // 2) as i:
        body(2 * i, 0, i)
        body(2 * i + 1, 1, i)


def build(nc, x, src, dst, wT, vecs, consts, out, h1, x1, sums):
    with ExitStack() as ctx:
        def sb(name, shape, dt=F32):
            return ctx.enter_context(nc.sbuf_tensor(name, shape, dt))

        def pb(name, shape, dt=F32):
            return ctx.enter_context(nc.psum_tensor(name, shape, dt))

        def sem(name):
            return ctx.enter_context(nc.semaphore(name))

        cst = sb("cst", [128, C_ALL])
        w = sb("w", [128, 2, 2, KC, D])
        vec = sb("vec", [128, 6, D])
        ident = cst[:, C_ID:C_ID + 128]
        iota = cst[:, C_IOTA:C_IOTA + 128]
        ones = cst[:, C_ONE:C_ONE + 128]
        dall = sb("dall", [125, ER + 1], I32)
        dallf = sb("dallf", [125, ER + 1])
        before = sb("before", [125, 128])
        rowf = sb("rowf", [128, 1])
        rowi = sb("rowi", [128, 1], I32)
        drow = sb("drow", [128, ER], I32)
        drowf = sb("drowf", [128, ER])
        drowl = sb("drowl", [128, ER])
        below = sb("below", [128, 1])
        far = sb("far", [128, 1])
        startc = sb("startc", [128, 1])
        falls = sb("falls", [125, 1])
        startr = sb("startr", [1, NT])
        starti = sb("starti", [1, NT], I32)
        length = sb("length", [1, NT])
        longest = sb("longest", [1, 1])
        flags = sb("flags", [1, 3])
        flagi = sb("flagi", [1, 1], I32)
        base = sb("base", [128, NT])
        wsrc = sb("wsrc", [128, NT * CH], I32)
        wdst = sb("wdst", [128, NT * CH], I32)
        idx = sb("idx", [128, 2, CH], I32)
        key = sb("key", [128, 2, CH])
        hot = sb("hot", [128, 2, CH, 128])
        rows = sb("rows", [128, CH, D])
        xs = sb("xs", [128, 2, D])
        xr = sb("xr", [128, 2, D])
        xT = sb("xT", [128, 2, KC, 128])
        agg = sb("agg", [128, 2, D])
        aT = sb("aT", [128, 2, KC, 128])
        ext = sb("ext", [125, DX])
        cntm = sb("cntm", [128, 2])
        rcnt = sb("rcnt", [128, 2])
        rcall = sb("rcall", [128, NT])
        hb = sb("hb", [128, D])
        hn = sb("hn", [128, D])
        hg = sb("hg", [128, D])
        ha = sb("ha", [128, D])
        u = sb("u", [128, D])
        st = sb("st", [128, 2, 6])
        mv = sb("mv", [128, 2, 2])
        sd = sb("sd", [128, 3])
        rstd = sb("rstd", [128, 4])
        x1o = sb("x1o", [128, 2, D])
        hs = sb("hs", [128, D])
        h1o = sb("h1o", [128, 2, D])
        gi = sb("gi", [125, 2], I32)
        gf = sb("gf", [125, 1])
        grow = sb("grow", [125, DX])
        gold = sb("gold", [125, DX])
        same = sb("same", [125, 125])
        mask = sb("mask", [125, 125])
        rank = sb("rank", [125, 3])
        gto = sb("gto", [125, 1], I32)
        psA = pb("psA", [128, D])
        psC = pb("psC", [128, 2, D // 2])
        psX = pb("psX", [128, KC, 128])
        psT = pb("psT", [128, KC, 128])
        psH = pb("psH", [128, 2, D])
        psS = pb("psS", [128, D])

        s_const, s_w, s_vec, s_dall = sem("s_const"), sem("s_w"), sem("s_vec"), sem("s_dall")
        s_pad, s_drow, s_tick, s_link = sem("s_pad"), sem("s_drow"), sem("s_tick"), sem("s_link")
        s_before, s_rowi, s_startc, s_falls, s_flagr, s_flag = [sem("s_" + n) for n in ("before", "rowi", "startc", "falls", "flagr", "flag")]
        s_pcount, s_pstart, s_pfalls, s_pflag = [sem("s_p" + n) for n in ("count", "start", "falls", "flag")]
        s_win = [sem(f"s_win{k}") for k in range(2)]
        s_idx = sem("s_idx")
        s_desc = sem("s_desc")
        s_row = [sem(f"s_row{c}") for c in range(CH)]
        s_used = sem("s_used")
        s_key, s_hot = sem("s_key"), sem("s_hot")
        s_xs = [sem(f"s_xs{k}") for k in range(2)]
        s_xt, s_xT = sem("s_xt"), sem("s_xT")
        s_cnt, s_rc, s_rca = sem("s_cnt"), sem("s_rc"), sem("s_rca")
        s_agg, s_at, s_aT = sem("s_agg"), sem("s_at"), sem("s_aT")
        s_ext, s_extu = sem("s_ext"), sem("s_extu")
        s_h = sem("s_h")
        s_hb, s_st, s_mv, s_rs, s_hn, s_hg, s_ha, s_u = [sem("s_" + n) for n in ("hb", "st", "mv", "rs", "hn", "hg", "ha", "u")]
        s_st2, s_mv2, s_rs2, s_x1, s_v1, s_rs3, s_hs, s_h1 = [sem("s_" + n) for n in ("st2", "mv2", "rs2", "x1", "v1", "rs3", "hs", "h1")]
        s_sd, s_sd2, s_sd3 = sem("s_sd"), sem("s_sd2"), sem("s_sd3")
        s_stx = [sem(f"s_stx{k}") for k in range(2)]
        s_sth = [sem(f"s_sth{k}") for k in range(2)]

        s_base, s_extz, s_zero, s_gi, s_gr, s_gf, s_gd, s_same, s_gs, s_gnew, s_gto, s_gout, s_gone = [
            sem("s_" + n) for n in ("base", "extz", "zero", "gi", "gr", "gf", "gd", "same", "gs", "gnew", "gto", "gout", "gone")]
        s_gstep = sem("s_gstep")

        block = ctx.enter_context(nc.Block())
        table = [x, h1]
        T = NT

        @block.sync
        def _(sp):
            sp.dma_start(cst[:, :], consts).then_inc(s_const, 16)
            sp.dma_start(dall[:, 0:ER], dst.rearrange("(p e) -> p e", p=125)).then_inc(s_dall, 16)
            sp.wait_ge(s_pad, 1)
            with nc.allow_non_contiguous_dma(reason="one column of the next row's first edges"):
                sp.dma_start(dall[0:124, ER:ER + 1],
                             dst.rearrange("(p e) -> p e", p=125)[1:125, 0:1]).then_inc(s_dall, 16)
            sp.dma_start(vec[:, :, :], vecs.rearrange("p (v d) -> p v d", v=6)).then_inc(s_vec, 16)
            sp.dma_start(w[:, :, :, :, :].rearrange("p l s c d -> p (l s c d)"), wT).then_inc(s_w, 16)
            sp.wait_ge(s_flag, 1)
            flag = sp.value_load(flagi[0:1, 0:1], min_val=0, max_val=1)

            def load_window(t, k, j):
                hold(sp, s_win[k], 32 * j, s_tick)
                at = sp.value_load(starti[0:1, bass.ds(t, 1)], min_val=0, max_val=E - CAP)
                sp.dma_start(wsrc[:, bass.ds(t * CH, CH)],
                             src[bass.ds(at, CAP)].rearrange("(p c) -> p c", c=CH)).then_inc(s_win[k], 16)
                sp.dma_start(wdst[:, bass.ds(t * CH, CH)],
                             dst[bass.ds(at, CAP)].rearrange("(p c) -> p c", c=CH)).then_inc(s_win[k], 16)

            for L in range(2):
                def load_rows(t, k, j):
                    hold(sp, s_u, t + L * T - 1, s_tick)
                    hold(sp, s_xt, t + L * T - 1, s_tick)
                    sp.dma_start(xs[0:PN, k, :], table[L][bass.ds(t * PN, PN), :]).then_inc(s_xs[k], 16)
                    if L == 1:
                        sp.dma_start(xr[0:PN, k, :], x1[bass.ds(t * PN, PN), :]).then_inc(s_xs[k], 16)

                def tile(t, k, j):
                    if L == 0:
                        load_window(t, k, j)
                    load_rows(t, k, j)
                    with sp.If(flag):
                        hold(sp, s_extu, t + L * T, s_tick)
                        sp.dma_start(ext[:, :], sums[bass.ds(t * PN, PN), :]).then_inc(s_ext, 16)

                def store(t, k, j):
                    hold(sp, s_x1, t + L * T + 1, s_tick)
                    sp.dma_start((x1 if L == 0 else out)[bass.ds(t * PN, PN), :], x1o[0:PN, k, :]).then_inc(s_stx[k], 16)
                    if L == 0:
                        hold(sp, s_h1, t + 1, s_tick)
                        sp.dma_start(h1[bass.ds(t * PN, PN), :], h1o[0:PN, k, :]).then_inc(s_sth[k], 16)

                if L == 1:
                    for k in range(2):
                        sp.wait_ge(s_sth[k], 16 * (NT // 2))
                        sp.wait_ge(s_stx[k], 16 * (NT // 2))
                with sp.If(flag):
                    if L == 0:
                        sp.wait_ge(s_extz, 1)
                    else:
                        sp.wait_ge(s_ext, 16 * NT)
                        sp.wait_ge(s_extz, 2)
                    with sp.Fori(0, NT + 1) as i:
                        sp.dma_start(sums[bass.ds(i * PN, PN), :], ext[:, :]).then_inc(s_zero, 16)
                        hold(sp, s_zero, 16 * (i + 1 + L * (NT + 1)), s_tick)
                    with sp.Fori(0, GT) as g:
                        sp.dma_start(gi[:, 0:1], src[bass.ds(g * 125, 125)].rearrange("(p c) -> p c", c=1)).then_inc(s_gi, 16)
                        sp.dma_start(gi[:, 1:2], dst[bass.ds(g * 125, 125)].rearrange("(p c) -> p c", c=1)).then_inc(s_gi, 16)
                        hold(sp, s_gone, g + L * GT + 1, s_tick)
                tile(0, 0, 0)
                tile(1, 1, 0)
                store(0, 0, 0)
                with sp.Fori(1, NT // 2) as i:
                    tile(2 * i, 0, i)
                    store(2 * i - 1, 1, i - 1)
                    tile(2 * i + 1, 1, i)
                    store(2 * i, 0, i)
                store(NT - 1, 1, NT // 2 - 1)
            for k in range(2):
                sp.wait_ge(s_stx[k], 16 * NT)

        @block.gpsimd
        def _(pool):
            pool.memset(dall[:, ER:ER + 1], 1 << 20).then_inc(s_pad, 1)
            hold(pool, s_rowi, 1, s_tick)
            pool.indirect_dma_start(drow[:, :], None, dst.rearrange("(p e) -> p e", p=125),
                                    bass.IndirectOffsetOnAxis(ap=rowi[:, 0:1], axis=0)).then_inc(s_drow, 16)
            hold(pool, s_flag, 1, s_tick)
            flag = pool.value_load(flagi[0:1, 0:1], min_val=0, max_val=1)
            for L in range(2):
                if L == 1:
                    for k in range(2):
                        hold(pool, s_sth[k], 16 * (NT // 2), s_tick)

                with pool.If(flag):
                    hold(pool, s_zero, 16 * (NT + 1) * (L + 1), s_tick)
                    with pool.Fori(0, GT) as g:
                        n = g + L * GT
                        hold(pool, s_gi, 32 * (n + 1), s_tick)
                        pool.indirect_dma_start(grow[:, 0:D], None, table[L],
                                                bass.IndirectOffsetOnAxis(ap=gi[:, 0:1], axis=0)).then_inc(s_gr, 16)
                        pool.indirect_dma_start(gold[:, :], None, sums,
                                                bass.IndirectOffsetOnAxis(ap=gi[:, 1:2], axis=0)).then_inc(s_gr, 16)
                        hold(pool, s_gnew, n + 1, s_tick)
                        hold(pool, s_gto, n + 1, s_tick)
                        pool.indirect_dma_start(sums, bass.IndirectOffsetOnAxis(ap=gto[:, 0:1], axis=0),
                                                gold[:, :], None).then_inc(s_gout, 16)
                        hold(pool, s_gout, 16 * (n + 1), s_tick)
                        pool.sem_inc(s_gone, 1)

                def tile(t, k, j):
                    if L == 0:
                        hold(pool, s_win[k], 32 * (j + 1), s_tick)
                    hold(pool, s_desc, (t + L * T - 1) * CH, s_tick)
                    pool.tensor_copy(idx[:, k, :], wsrc[:, bass.ds(t * CH, CH)]).then_inc(s_idx, 1)
                    hold(pool, s_idx, t + L * T + 1, s_tick)
                    for c in range(CH):
                        hold(pool, s_used, (t + L * T - 1) * CH + c + 1, s_tick)
                        pool.indirect_dma_start(rows[:, c, :], None, table[L],
                                                bass.IndirectOffsetOnAxis(ap=idx[:, k, c:c + 1], axis=0),
                                                engine_sem=s_desc).then_inc(s_row[c], 16)

                over_tiles(pool, tile)

        @block.tensor
        def _(pe):
            pe.wait_ge(s_const, 16)
            pe.wait_ge(s_before, 1)
            pe.matmul(psS[:, 0:1], before[:, :], ones[0:125, 0:1], start=True, stop=True).then_inc(s_pcount, 1)
            pe.wait_ge(s_startc, 1)
            pe.matmul(psA[0:1, 0:128], startc[:, :], ident, start=True, stop=True).then_inc(s_pstart, 1)
            pe.wait_ge(s_falls, 1)
            pe.matmul(psT[0:1, 0, 0:1], falls[:, :], ones[0:125, 0:1], start=True, stop=True).then_inc(s_pfalls, 1)
            pe.wait_ge(s_flagr, 1)
            pe.matmul(psX[:, 0, 0:1], ones[0:1, :], flags[:, 2:3], start=True, stop=True).then_inc(s_pflag, 1)
            pe.wait_ge(s_flag, 1)
            flag = pe.value_load(flagi[0:1, 0:1], min_val=0, max_val=1)
            pe.wait_ge(s_w, 16)
            pe.wait_ge(s_base, 1)
            for L in range(2):
                with pe.If(flag):
                    with pe.Fori(0, GT) as g:
                        n = g + L * GT
                        pe.wait_ge(s_gf, n + 1)
                        pe.matmul(psS[0:125, 0:125], gf[:, 0:1].to_broadcast([125, 125]), ident[0:125, 0:125],
                                  start=True, stop=True).then_inc(s_gd, 1)
                        pe.wait_ge(s_same, n + 1)
                        pe.wait_ge(s_gr, 32 * (n + 1))
                        pe.matmul(psX[0:125, 0, 0:2], same[:, :], grow[:, D:DX], start=True, stop=True)
                        pe.matmul(psA[0:125, :], same[:, :], grow[:, 0:D], start=True, stop=True).then_inc(s_gs, 1)

                def tile(t, k, j):
                    n = t + L * T

                    def dense(src_sb, s, c, first, last):
                        return pe.matmul(psH[0:PN, k, :], src_sb[:, k, c, 0:PN], w[:, L, s, c, :],
                                         start=first, stop=last)

                    pe.wait_ge(s_hot, n + 1)
                    if L == 0:
                        wait(pe, s_cnt, n - 1)
                    for c in range(CH):
                        pe.wait_ge(s_row[c], 16 * (n + 1))
                        if L == 0:
                            pe.matmul(psC[0:PN, k, 0:1], hot[:, k, c, 0:PN], ones[:, 0:1],
                                      start=(c == 0), stop=(c == CH - 1))
                        if c == CH - 1:
                            with pe.If(flag):
                                pe.wait_ge(s_ext, 16 * (n + 1))
                                if L == 0:
                                    pe.matmul(psC[0:PN, k, 0:1], ident[0:PN, 0:PN], ext[:, D:D + 1],
                                              start=False, stop=False, skip_group_check=True)
                                pe.matmul(psA[0:PN, :], ident[0:PN, 0:PN], ext[:, 0:D], start=False, stop=False,
                                          skip_group_check=True).then_inc(s_extu, 1)
                        pe.matmul(psA[0:PN, :], hot[:, k, c, 0:PN], rows[:, c, :], start=(c == 0),
                                  stop=(c == CH - 1)).then_inc(s_used, 1)
                        if c == CH - 3:
                            pe.wait_ge(s_xs[k], 16 * (j + 1) if L == 0 else 16 * (NT // 2) + 32 * (j + 1))
                            wait(pe, s_xT, n)
                            for q in range(KC):
                                m = pe.transpose(psX[:, q, 0:PN], xs[0:PN, k, q * 128:(q + 1) * 128], ident[0:PN, 0:PN])
                            m.then_inc(s_xt, 1)
                    pe.wait_ge(s_xT, n + 1)
                    wait(pe, s_hb, n - 1)
                    dense(xT, 0, 0, True, False)
                    dense(xT, 0, 1, False, False)
                    pe.wait_ge(s_agg, n + 1)
                    for q in range(KC):
                        m = pe.transpose(psT[:, q, 0:PN], agg[0:PN, k, q * 128:(q + 1) * 128], ident[0:PN, 0:PN])
                    m.then_inc(s_at, 1)
                    dense(xT, 0, 2, False, False)
                    dense(xT, 0, 3, False, False)
                    pe.wait_ge(s_aT, n + 1)
                    for c in range(KC):
                        m = dense(aT, 1, c, False, c == KC - 1)
                    m.then_inc(s_h, 1)

                over_tiles(pe, tile)

        @block.scalar
        def _(act):
            act.wait_ge(s_const, 16)
            for L in range(2):
                def tile(t, k, j):
                    n = t + L * T
                    act.wait_ge(s_xt, n + 1)
                    act.activation(xT[:, k, :, 0:PN], psX[:, :, 0:PN], ACT.Copy).then_inc(s_xT, 1)
                    act.wait_ge(s_used, CH * (n + 1))
                    act.wait_ge(s_rc, n + 1)
                    act.activation(agg[0:PN, k, :], psA[0:PN, :], ACT.Copy, scale=rcnt[0:PN, k:k + 1]).then_inc(s_agg, 1)
                    act.wait_ge(s_at, n + 1)
                    act.activation(aT[:, k, :, 0:PN], psT[:, :, 0:PN], ACT.Copy).then_inc(s_aT, 1)

                def deviations(t, k, j):
                    n = t + L * T
                    eps = cst[0:PN, C_EPS:C_EPS + 1]
                    if L == 0:
                        act.wait_ge(s_mv, n + 1)
                        act.activation(sd[0:PN, 0:1], mv[0:PN, 0, 1:2], ACT.Sqrt, bias=eps).then_inc(s_sd, 1)
                    act.wait_ge(s_mv2, n + 1)
                    act.activation(sd[0:PN, 1:2], mv[0:PN, 1, 1:2], ACT.Sqrt, bias=eps).then_inc(s_sd2, 1)
                    if L == 0:
                        act.wait_ge(s_v1, n + 1)
                        act.activation(sd[0:PN, 2:3], rstd[0:PN, 2:3], ACT.Sqrt, bias=eps).then_inc(s_sd3, 1)

                tile(0, 0, 0)
                deviations(0, 0, 0)
                tile(1, 1, 0)
                with act.Fori(1, NT // 2) as i:
                    deviations(2 * i - 1, 1, i - 1)
                    tile(2 * i, 0, i)
                    deviations(2 * i, 0, i)
                    tile(2 * i + 1, 1, i)
                deviations(NT - 1, 1, NT // 2 - 1)

        @block.vector
        def _(v):
            linked = [0]

            def link(ins):
                linked[0] += 1
                ins.then_inc(s_link, 1)
                v.wait_ge(s_link, linked[0])

            link(v.memset(grow[:, D:DX], 1.0))
            v.wait_ge(s_const, 16)
            v.wait_ge(s_dall, 32)
            link(v.tensor_copy(dallf[:, :], dall[:, :]))
            v.tensor_scalar(before[:, :], cst[0:125, C_THR:C_THR + 128], dallf[:, ER - 1:ER], None,
                            ALU.is_gt).then_inc(s_before, 1)
            v.wait_ge(s_pcount, 1)
            link(v.tensor_scalar(rowf[:, :], psS[:, 0:1], 124.0, None, ALU.min))
            v.tensor_copy(rowi[:, :], rowf[:, :]).then_inc(s_rowi, 1)
            v.wait_ge(s_drow, 16)
            link(v.tensor_copy(drowf[:, :], drow[:, :]))
            link(v.tensor_scalar(drowl[:, :], drowf[:, :], cst[:, C_THRC:C_THRC + 1], None, ALU.is_lt))
            link(v.tensor_reduce(below[:, :], drowl[:, :], AX_X, ALU.add))
            v.scalar_tensor_tensor(out=startc[:, :], in0=rowf[:, :], scalar=float(ER), in1=below[:, :],
                                   op0=ALU.mult, op1=ALU.add).then_inc(s_startc, 1)
            link(v.tensor_tensor(drowf[0:125, :], dallf[:, 0:ER], dallf[:, 1:ER + 1], ALU.is_gt))
            v.tensor_reduce(falls[:, :], drowf[0:125, :], AX_X, ALU.add).then_inc(s_falls, 1)
            v.wait_ge(s_pstart, 1)
            link(v.tensor_scalar(startr[:, :], psA[0:1, 0:NT], float(E - CAP), None, ALU.min))
            link(v.tensor_copy(starti[:, :], startr[:, :]))
            link(v.tensor_tensor(length[:, :], psA[0:1, HI:HI + NT], startr[:, :], ALU.subtract))
            link(v.tensor_reduce(longest[:, :], length[:, :], AX_X, ALU.max))
            v.wait_ge(s_pfalls, 1)
            link(v.tensor_scalar(flags[:, 0:1], psT[0:1, 0, 0:1], 0.5, None, ALU.is_gt))
            link(v.tensor_scalar(flags[:, 1:2], longest[:, :], CAP + 0.5, None, ALU.is_gt))
            v.tensor_tensor(flags[:, 2:3], flags[:, 0:1], flags[:, 1:2], ALU.max).then_inc(s_flagr, 1)
            v.wait_ge(s_flagr, 1)
            v.tensor_copy(flagi[:, :], flags[:, 2:3]).then_inc(s_flag, 1)
            v.wait_ge(s_pflag, 1)
            link(v.tensor_scalar(far[:, :], psX[:, 0, 0:1], FAR, None, ALU.mult))
            v.tensor_scalar(base[:, :], cst[:, C_BASE:C_BASE + NT], far[:, 0:1], None, ALU.add).then_inc(s_base, 1)
            v.wait_ge(s_base, 1)
            v.wait_ge(s_flag, 1)
            flag = v.value_load(flagi[0:1, 0:1], min_val=0, max_val=1)
            v.wait_ge(s_vec, 16)

            def general(L):
                v.memset(ext[:, :], 0.0).then_inc(s_extz, 1)
                with v.Fori(0, GT) as g:
                    n = g + L * GT
                    v.wait_ge(s_gi, 32 * (n + 1))
                    v.tensor_copy(gf[:, :], gi[:, 1:2]).then_inc(s_gf, 1)
                    v.wait_ge(s_gd, n + 1)
                    v.tensor_scalar(same[:, :], psS[0:125, 0:125], gf[:, 0:1], None, ALU.is_equal).then_inc(s_same, 1)
                    v.wait_ge(s_same, n + 1)
                    v.tensor_tensor(mask[:, :], same[:, :], cst[0:125, C_TRI:C_TRI + 125], ALU.mult).then_inc(s_gstep, 1)
                    v.wait_ge(s_gstep, 5 * n + 1)
                    v.tensor_reduce(rank[:, 0:1], mask[:, :], AX_X, ALU.max).then_inc(s_gstep, 1)
                    v.tensor_tensor(rank[:, 1:2], cst[0:125, C_DUMP:C_DUMP + 1], gf[:, :], ALU.subtract).then_inc(s_gstep, 1)
                    v.wait_ge(s_gstep, 5 * n + 3)
                    v.tensor_tensor(rank[:, 2:3], rank[:, 0:1], rank[:, 1:2], ALU.mult).then_inc(s_gstep, 1)
                    v.wait_ge(s_gstep, 5 * n + 4)
                    v.tensor_tensor(gto[:, :], rank[:, 2:3], gf[:, :], ALU.add).then_inc(s_gto, 1)
                    v.wait_ge(s_gs, n + 1)
                    v.tensor_tensor(gold[:, D:DX], gold[:, D:DX], psX[0:125, 0, 0:2], ALU.add).then_inc(s_gstep, 1)
                    v.wait_ge(s_gstep, 5 * n + 5)
                    v.tensor_tensor(gold[:, 0:D], gold[:, 0:D], psA[0:125, :], ALU.add).then_inc(s_gnew, 1)

            for L in range(2):
                if L == 1:
                    v.wait_ge(s_used, CH * NT)
                with v.If(flag):
                    if L == 1:
                        v.wait_ge(s_extu, NT)
                    general(L)

                def keys(t, k, j):
                    n = t + L * T
                    if L == 0:
                        v.wait_ge(s_win[k], 32 * (j + 1))
                    wait(v, s_used, (n - 1) * CH)
                    v.tensor_tensor(key[:, k, :], wdst[:, bass.ds(t * CH, CH)],
                                    base[:, bass.ds(t, 1)].to_broadcast([128, CH]), ALU.subtract).then_inc(s_key, 1)
                    v.wait_ge(s_key, n + 1)
                    v.tensor_tensor(hot[:, k, :, :], iota.unsqueeze(1).to_broadcast([128, CH, 128]),
                                    key[:, k, :].unsqueeze(2).to_broadcast([128, CH, 128]), ALU.is_equal).then_inc(s_hot, 1)

                def normal(b, src_sb, s_in, s_stats, s_mvs, s_dev, s_out, n):
                    v.wait_ge(s_in, n + 1)
                    v.bn_stats(st[0:PN, b, :], src_sb).then_inc(s_stats, 1)
                    hold(v, s_stats, n + 1, s_tick)
                    v.bn_aggr(mv[0:PN, b, :], st[0:PN, b, :]).then_inc(s_mvs, 1)
                    v.wait_ge(s_dev, n + 1)
                    v.reciprocal(rstd[0:PN, b:b + 1], sd[0:PN, b:b + 1]).then_inc(s_out, 1)
                    v.wait_ge(s_out, n + 1)

                def tile(t, k, j):
                    n = t + L * T
                    x_k = xs[0:PN, k, :]
                    if L == 0:
                        v.wait_ge(s_used, CH * (n + 1))
                        v.tensor_scalar(cntm[0:PN, k:k + 1], psC[0:PN, k, 0:1], 1.0, None, ALU.max).then_inc(s_cnt, 1)
                        v.wait_ge(s_cnt, n + 1)
                        v.reciprocal(rcnt[0:PN, k:k + 1], cntm[0:PN, k:k + 1]).then_inc(s_rc, 1)
                        v.wait_ge(s_rc, n + 1)
                        v.tensor_scalar(rcall[0:PN, bass.ds(t, 1)], rcnt[0:PN, k:k + 1], 1.0, None,
                                        ALU.mult).then_inc(s_rca, 1)
                    else:
                        v.wait_ge(s_rca, NT)
                        v.wait_ge(s_agg, n - 1)
                        v.tensor_scalar(rcnt[0:PN, k:k + 1], rcall[0:PN, bass.ds(t, 1)], 1.0, None,
                                        ALU.mult).then_inc(s_rc, 1)
                    mv0, mv1 = mv[0:PN, 0, :], mv[0:PN, 1, :]
                    if L == 0:
                        v.wait_ge(s_h, n + 1)
                        wait(v, s_hn, n)
                        v.tensor_tensor(hb[0:PN, :], psH[0:PN, k, :], vec[0:PN, 0, :], ALU.add).then_inc(s_hb, 1)
                        normal(0, hb[0:PN, :], s_hb, s_st, s_mv, s_sd, s_rs, n)
                        v.tensor_scalar(hn[0:PN, :], hb[0:PN, :], mv0[:, 0:1], rstd[0:PN, 0:1],
                                        ALU.subtract, ALU.mult).then_inc(s_hn, 1)
                        v.wait_ge(s_hn, n + 1)
                        v.tensor_tensor(hg[0:PN, :], hn[0:PN, :], vec[0:PN, 1, :], ALU.mult).then_inc(s_hg, 1)
                        v.wait_ge(s_hg, n + 1)
                        v.tensor_tensor(ha[0:PN, :], hg[0:PN, :], vec[0:PN, 2, :], ALU.add).then_inc(s_ha, 1)
                        v.wait_ge(s_ha, n + 1)
                        v.scalar_tensor_tensor(out=u[0:PN, :], in0=ha[0:PN, :], scalar=0.0, in1=x_k,
                                               op0=ALU.max, op1=ALU.add).then_inc(s_u, 1)
                    else:
                        v.wait_ge(s_h, n + 1)
                        v.wait_ge(s_ha, n)
                        v.tensor_tensor(hb[0:PN, :], psH[0:PN, k, :], vec[0:PN, 5, :], ALU.add).then_inc(s_hb, 1)
                        v.wait_ge(s_hb, n + 1)
                        v.wait_ge(s_xs[k], 16 * (NT // 2) + 32 * (j + 1))
                        v.scalar_tensor_tensor(out=ha[0:PN, :], in0=hb[0:PN, :], scalar=0.0, in1=xr[0:PN, k, :],
                                               op0=ALU.max, op1=ALU.add).then_inc(s_ha, 1)
                        v.wait_ge(s_ha, n + 1)
                        v.tensor_tensor(u[0:PN, :], ha[0:PN, :], xr[0:PN, k, :], ALU.add).then_inc(s_u, 1)
                    normal(1, u[0:PN, :], s_u, s_st2, s_mv2, s_sd2, s_rs2, n)
                    wait(v, s_stx[k], 16 * (j + L * (NT // 2)))
                    v.tensor_scalar(x1o[0:PN, k, :], u[0:PN, :], mv1[:, 0:1], rstd[0:PN, 1:2],
                                    ALU.subtract, ALU.mult).then_inc(s_x1, 1)
                    if L == 0:
                        v.tensor_scalar(rstd[0:PN, 2:3], mv1[:, 1:2], rstd[0:PN, 1:2], rstd[0:PN, 1:2],
                                        ALU.mult, ALU.mult).then_inc(s_v1, 1)
                        v.wait_ge(s_sd3, n + 1)
                        v.reciprocal(rstd[0:PN, 3:4], sd[0:PN, 2:3]).then_inc(s_rs3, 1)
                        v.wait_ge(s_rs3, n + 1)
                        v.wait_ge(s_x1, n + 1)
                        v.scalar_tensor_tensor(out=hs[0:PN, :], in0=x1o[0:PN, k, :], scalar=rstd[0:PN, 3:4],
                                               in1=vec[0:PN, 3, :], op0=ALU.mult, op1=ALU.mult).then_inc(s_hs, 1)
                        v.wait_ge(s_hs, n + 1)
                        wait(v, s_sth[k], 16 * j)
                        v.tensor_tensor(h1o[0:PN, k, :], hs[0:PN, :], vec[0:PN, 4, :], ALU.add).then_inc(s_h1, 1)

                keys(0, 0, 0)
                keys(1, 1, 0)
                tile(0, 0, 0)
                with v.Fori(1, NT // 2) as i:
                    keys(2 * i, 0, i)
                    tile(2 * i - 1, 1, i - 1)
                    keys(2 * i + 1, 1, i)
                    tile(2 * i, 0, i)
                tile(NT - 1, 1, NT // 2 - 1)


def kernel(x, src, dst, L0_gnn_w_self, L0_gnn_w_neigh, L0_gnn_bias, L0_gnn_gamma, L0_gnn_beta,
           L1_gnn_W_l, L1_gnn_b_l, L1_gnn_W_r, L1_gnn_gamma, L1_gnn_beta):
    import numpy as np
    import concourse.bacc as bacc
    from concourse.bass_utils import run_bass_kernel_spmd

    w = np.stack([np.asarray(a) for a in (L0_gnn_w_self, L0_gnn_w_neigh, L1_gnn_W_r, L1_gnn_W_l)])
    w = w.reshape(2, 2, D, KC, 128).transpose(4, 0, 1, 3, 2)
    vecs = np.stack([np.asarray(a) for a in (L0_gnn_bias, L0_gnn_gamma, L0_gnn_beta, L1_gnn_gamma, L1_gnn_beta,
                                             L1_gnn_b_l)])
    arrays = {
        "x": np.ascontiguousarray(x), "src": np.ascontiguousarray(src), "dst": np.ascontiguousarray(dst),
        "wT": np.ascontiguousarray(w.reshape(128, 4 * KC * D)),
        "vecs": np.ascontiguousarray(np.broadcast_to(vecs.reshape(1, 6 * D), (128, 6 * D))),
        "consts": constants(np),
    }
    nc = bacc.Bacc("TRN2", target_bir_lowering=False, num_devices=1)
    ins = [nc.dram_tensor(n, a.shape, mybir.dt.from_np(a.dtype), kind="ExternalInput").ap() for n, a in arrays.items()]
    out = nc.dram_tensor("out", (N, D), F32, kind="ExternalOutput").ap()
    h1 = nc.dram_tensor("h1", (N, D), F32, kind="Internal").ap()
    x1 = nc.dram_tensor("x1", (N, D), F32, kind="Internal").ap()
    sums = nc.dram_tensor("sums", (N + PN, DX), F32, kind="Internal").ap()
    build(nc, *ins, out, h1, x1, sums)
    r = run_bass_kernel_spmd(nc, [arrays], core_ids=[0])
    return r.results[0]["out"]
```

```python
from contextlib import ExitStack

import concourse.bass as bass
from concourse import mybir

F32 = mybir.dt.float32
F32R = mybir.dt.float32r
I32 = mybir.dt.int32
ALU = mybir.AluOpType
ACT = mybir.ActivationFunctionType
AX_X = mybir.AxisListType.X

N, E, D = 6250, 100000, 512
EPS = 1e-5
PN = 125
NT = N // PN
CH = 17
CAP = CH * 128
KC = D // 128
WHOLE = (0, 1, 3, 4)
SPLIT = tuple(c for c in range(CH) if c not in WHOLE)
NS = len(SPLIT)
PARTS = 6
ER = E // 125
GT = E // 125
HI = 64
FAR = 1.0e6
DX = D + 2

C_ID, C_IOTA, C_THR, C_TRI, C_ONE = 0, 128, 256, 384, 512
C_THRC, C_BASE, C_DUMP = 640, 641, 641 + NT
C_EPS = C_DUMP + 1
C_ALL = C_EPS + 1


def constants(np):
    c = np.zeros((128, C_ALL), np.float32)
    p = np.arange(128)
    c[:, C_ID:C_ID + 128] = np.eye(128)
    c[:, C_IOTA:C_IOTA + 128] = p
    thr = np.where(p < HI, PN * p, PN * (p - HI + 1))
    c[:, C_THR:C_THR + 128] = thr
    c[:, C_TRI:C_TRI + 128] = p[None, :] < p[:, None]
    c[:, C_ONE:C_ONE + 128] = 1.0
    c[:, C_THRC] = thr
    c[:, C_BASE:C_BASE + NT] = PN * np.arange(NT)
    c[:, C_DUMP] = N + p
    c[:, C_EPS] = EPS
    return c


def wait(eng, sem, value):
    if not isinstance(value, int) or value > 0:
        eng.wait_ge(sem, value)


def hold(eng, sem, value, tick):
    wait(eng, sem, value)
    if not isinstance(value, int):
        eng.sem_inc(tick, 1)


def over_periods(eng, period):
    period(0, 0, 0, -1, True, False, False)
    period(1, 1, 0, 0, True, True, False)
    with eng.Fori(1, NT // 2) as i:
        period(2 * i, 0, i, i - 1, True, True, True)
        period(2 * i + 1, 1, i, i, True, True, True)
    period(NT, 0, NT // 2, NT // 2 - 1, False, True, True)
    period(NT + 1, 1, NT // 2, NT // 2, False, False, True)


def last_in_slot(n, i):
    if i >= PARTS:
        return n * CH + SPLIT[i - PARTS] + 1
    last = max(q for q in range(NS) if q % PARTS == i)
    return (n - 1) * CH + SPLIT[last] + 1


def build(nc, x, src, dst, wT, vecs, consts, out, h1, x1, sums):
    with ExitStack() as ctx:
        def sb(name, shape, dt=F32):
            return ctx.enter_context(nc.sbuf_tensor(name, shape, dt))

        def pb(name, shape, dt=F32):
            return ctx.enter_context(nc.psum_tensor(name, shape, dt))

        def sem(name):
            return ctx.enter_context(nc.semaphore(name))

        cst = sb("cst", [128, C_ALL])
        w = sb("w", [128, 2, 2, KC, D])
        vec = sb("vec", [128, 6, D])
        ident = cst[:, C_ID:C_ID + 128]
        iota = cst[:, C_IOTA:C_IOTA + 128]
        ones = cst[:, C_ONE:C_ONE + 128]
        rows = sb("rows", [128, CH, D])
        scratch = rows[:, :, :].rearrange("p c d -> p (c d)")
        dall = sb("dall", [125, ER + 1], I32)
        dallf = scratch[0:125, 0:ER + 1]
        before = sb("before", [125, 128])
        rowf = sb("rowf", [128, 1])
        rowi = sb("rowi", [128, 1], I32)
        drow = sb("drow", [128, ER], I32)
        drowf, drowl = scratch[:, 1024:1024 + ER], scratch[:, 2048:2048 + ER]
        below = sb("below", [128, 1])
        far = sb("far", [128, 1])
        startc = sb("startc", [128, 1])
        falls = sb("falls", [125, 1])
        startr = sb("startr", [1, NT])
        starti = sb("starti", [1, NT + 2], I32)
        length = sb("length", [1, NT])
        longest = sb("longest", [1, 1])
        flags = sb("flags", [1, 3])
        flagi = sb("flagi", [1, 1], I32)
        base = sb("base", [128, NT])
        wsrc = sb("wsrc", [128, (NT + 2) * CH], I32)
        wdst = sb("wdst", [128, (NT + 2) * CH], I32)
        idx = sb("idx", [128, 2, CH], I32)
        key = sb("key", [128, 2, CH])
        hot = sb("hot", [128, CH, 128], F32R)
        high = sb("high", [128, PARTS, D], F32R)
        low = sb("low", [128, PARTS, D], F32R)
        ones2 = sb("ones2", [128, 2], F32R)
        xs = sb("xs", [128, 2, D])
        xr = sb("xr", [128, 2, D])
        xT = sb("xT", [128, 2, KC, 128])
        agg = sb("agg", [128, 2, D])
        aT = sb("aT", [128, 2, KC, 128])
        ext = sb("ext", [125, DX])
        cntm = sb("cntm", [128, 2])
        rcnt = sb("rcnt", [128, 2])
        rcall = sb("rcall", [128, NT])
        hb = sb("hb", [128, D])
        hn = sb("hn", [128, D])
        hg = sb("hg", [128, D])
        ha = sb("ha", [128, D])
        u = sb("u", [128, D])
        st = sb("st", [128, 2, 6])
        mv = sb("mv", [128, 2, 2])
        sd = sb("sd", [128, 3])
        rstd = sb("rstd", [128, 4])
        x1o = sb("x1o", [128, 2, D])
        hs = sb("hs", [128, D])
        h1o = sb("h1o", [128, 2, D])
        gi = sb("gi", [125, 2], I32)
        gf = sb("gf", [125, 1])
        grow = sb("grow", [125, DX])
        gold = sb("gold", [125, DX])
        same = sb("same", [125, 125])
        mask = sb("mask", [125, 125])
        rank = sb("rank", [125, 3])
        gto = sb("gto", [125, 1], I32)
        psA = pb("psA", [128, 2, D])
        psC = pb("psC", [128, 2, D])
        psX = pb("psX", [128, KC, 128])
        psT = pb("psT", [128, KC, 128])
        psH = pb("psH", [128, 2, D])

        s_const, s_w, s_vec, s_dall = sem("s_const"), sem("s_w"), sem("s_vec"), sem("s_dall")
        s_pad, s_drow, s_tick, s_link = sem("s_pad"), sem("s_drow"), sem("s_tick"), sem("s_link")
        s_before, s_rowi, s_startc, s_falls, s_flagr, s_flag = [sem("s_" + n) for n in ("before", "rowi", "startc", "falls", "flagr", "flag")]
        s_pcount, s_pstart, s_pfalls, s_pflag = [sem("s_p" + n) for n in ("count", "start", "falls", "flag")]
        s_win = [sem(f"s_win{k}") for k in range(2)]
        s_idx = sem("s_idx")
        s_desc = sem("s_desc")
        s_row = [sem(f"s_row{c}") for c in range(CH)]
        s_used = sem("s_used")
        s_high, s_low = sem("s_high"), sem("s_low")
        s_key, s_hot = sem("s_key"), sem("s_hot")
        s_xs = [sem(f"s_xs{k}") for k in range(2)]
        s_xt, s_xT = sem("s_xt"), sem("s_xT")
        s_cnt, s_rc, s_rca = sem("s_cnt"), sem("s_rc"), sem("s_rca")
        s_agg, s_at, s_aT = sem("s_agg"), sem("s_at"), sem("s_aT")
        s_ext, s_extu = sem("s_ext"), sem("s_extu")
        s_h = sem("s_h")
        s_hb, s_st, s_mv, s_rs, s_hn, s_hg, s_ha, s_u = [sem("s_" + n) for n in ("hb", "st", "mv", "rs", "hn", "hg", "ha", "u")]
        s_st2, s_mv2, s_rs2, s_x1, s_v1, s_rs3, s_hs, s_h1 = [sem("s_" + n) for n in ("st2", "mv2", "rs2", "x1", "v1", "rs3", "hs", "h1")]
        s_sd, s_sd2, s_sd3 = sem("s_sd"), sem("s_sd2"), sem("s_sd3")
        s_stx = [sem(f"s_stx{k}") for k in range(2)]
        s_sth = [sem(f"s_sth{k}") for k in range(2)]

        s_base, s_extz, s_zero, s_gi, s_gr, s_gf, s_gd, s_same, s_gs, s_gnew, s_gto, s_gout, s_gone = [
            sem("s_" + n) for n in ("base", "extz", "zero", "gi", "gr", "gf", "gd", "same", "gs", "gnew", "gto", "gout", "gone")]
        s_gstep = sem("s_gstep")

        block = ctx.enter_context(nc.Block())
        table = [x, h1]
        T = NT

        @block.sync
        def _(sp):
            sp.dma_start(cst[:, :], consts).then_inc(s_const, 16)
            sp.dma_start(dall[:, 0:ER], dst.rearrange("(p e) -> p e", p=125)).then_inc(s_dall, 16)
            sp.wait_ge(s_pad, 1)
            with nc.allow_non_contiguous_dma(reason="one column of the next row's first edges"):
                sp.dma_start(dall[0:124, ER:ER + 1],
                             dst.rearrange("(p e) -> p e", p=125)[1:125, 0:1]).then_inc(s_dall, 16)
            sp.dma_start(vec[:, :, :], vecs.rearrange("p (v d) -> p v d", v=6)).then_inc(s_vec, 16)
            sp.dma_start(w[:, :, :, :, :].rearrange("p l s c d -> p (l s c d)"), wT).then_inc(s_w, 16)
            sp.wait_ge(s_flag, 1)
            flag = sp.value_load(flagi[0:1, 0:1], min_val=0, max_val=1)

            def load_window(t, k, j):
                hold(sp, s_win[k], 32 * j, s_tick)
                at = sp.value_load(starti[0:1, bass.ds(t, 1)], min_val=0, max_val=E - CAP)
                sp.dma_start(wsrc[:, bass.ds(t * CH, CH)],
                             src[bass.ds(at, CAP)].rearrange("(p c) -> p c", c=CH)).then_inc(s_win[k], 16)
                sp.dma_start(wdst[:, bass.ds(t * CH, CH)],
                             dst[bass.ds(at, CAP)].rearrange("(p c) -> p c", c=CH)).then_inc(s_win[k], 16)

            load_window(0, 0, 0)
            load_window(1, 1, 0)
            for L in range(2):
                def load_rows(t, k, j):
                    hold(sp, s_u, t + L * T - 1, s_tick)
                    hold(sp, s_xt, t + L * T - 1, s_tick)
                    sp.dma_start(xs[0:PN, k, :], table[L][bass.ds(t * PN, PN), :]).then_inc(s_xs[k], 16)
                    if L == 1:
                        sp.dma_start(xr[0:PN, k, :], x1[bass.ds(t * PN, PN), :]).then_inc(s_xs[k], 16)

                def tile(t, k, j):
                    if L == 0:
                        load_window(t + 2, k, j + 1)
                    load_rows(t, k, j)
                    with sp.If(flag):
                        hold(sp, s_extu, t + L * T, s_tick)
                        sp.dma_start(ext[:, :], sums[bass.ds(t * PN, PN), :]).then_inc(s_ext, 16)

                def store(t, k, j):
                    hold(sp, s_x1, t + L * T + 1, s_tick)
                    sp.dma_start((x1 if L == 0 else out)[bass.ds(t * PN, PN), :], x1o[0:PN, k, :]).then_inc(s_stx[k], 16)
                    if L == 0:
                        hold(sp, s_h1, t + 1, s_tick)
                        sp.dma_start(h1[bass.ds(t * PN, PN), :], h1o[0:PN, k, :]).then_inc(s_sth[k], 16)

                if L == 1:
                    for k in range(2):
                        sp.wait_ge(s_sth[k], 16 * (NT // 2))
                        sp.wait_ge(s_stx[k], 16 * (NT // 2))
                with sp.If(flag):
                    if L == 0:
                        sp.wait_ge(s_extz, 1)
                    else:
                        sp.wait_ge(s_ext, 16 * NT)
                        sp.wait_ge(s_extz, 2)
                    with sp.Fori(0, NT + 1) as i:
                        sp.dma_start(sums[bass.ds(i * PN, PN), :], ext[:, :]).then_inc(s_zero, 16)
                        hold(sp, s_zero, 16 * (i + 1 + L * (NT + 1)), s_tick)
                    with sp.Fori(0, GT) as g:
                        sp.dma_start(gi[:, 0:1], src[bass.ds(g * 125, 125)].rearrange("(p c) -> p c", c=1)).then_inc(s_gi, 16)
                        sp.dma_start(gi[:, 1:2], dst[bass.ds(g * 125, 125)].rearrange("(p c) -> p c", c=1)).then_inc(s_gi, 16)
                        hold(sp, s_gone, g + L * GT + 1, s_tick)
                tile(0, 0, 0)
                tile(1, 1, 0)
                with sp.Fori(1, NT // 2) as i:
                    tile(2 * i, 0, i)
                    store(2 * i - 2, 0, i - 1)
                    tile(2 * i + 1, 1, i)
                    store(2 * i - 1, 1, i - 1)
                store(NT - 2, 0, NT // 2 - 1)
                store(NT - 1, 1, NT // 2 - 1)
            for k in range(2):
                sp.wait_ge(s_stx[k], 16 * NT)
                sp.wait_ge(s_win[k], 32 * (NT // 2 + 1))

        @block.gpsimd
        def _(pool):
            pool.memset(dall[:, ER:ER + 1], 1 << 20).then_inc(s_pad, 1)
            hold(pool, s_rowi, 1, s_tick)
            pool.indirect_dma_start(drow[:, :], None, dst.rearrange("(p e) -> p e", p=125),
                                    bass.IndirectOffsetOnAxis(ap=rowi[:, 0:1], axis=0)).then_inc(s_drow, 16)
            hold(pool, s_flag, 1, s_tick)
            flag = pool.value_load(flagi[0:1, 0:1], min_val=0, max_val=1)
            for L in range(2):
                if L == 1:
                    for k in range(2):
                        hold(pool, s_sth[k], 16 * (NT // 2), s_tick)

                with pool.If(flag):
                    hold(pool, s_zero, 16 * (NT + 1) * (L + 1), s_tick)
                    with pool.Fori(0, GT) as g:
                        n = g + L * GT
                        hold(pool, s_gi, 32 * (n + 1), s_tick)
                        pool.indirect_dma_start(grow[:, 0:D], None, table[L],
                                                bass.IndirectOffsetOnAxis(ap=gi[:, 0:1], axis=0)).then_inc(s_gr, 16)
                        pool.indirect_dma_start(gold[:, :], None, sums,
                                                bass.IndirectOffsetOnAxis(ap=gi[:, 1:2], axis=0)).then_inc(s_gr, 16)
                        hold(pool, s_gnew, n + 1, s_tick)
                        hold(pool, s_gto, n + 1, s_tick)
                        pool.indirect_dma_start(sums, bass.IndirectOffsetOnAxis(ap=gto[:, 0:1], axis=0),
                                                gold[:, :], None).then_inc(s_gout, 16)
                        hold(pool, s_gout, 16 * (n + 1), s_tick)
                        pool.sem_inc(s_gone, 1)

                def tile(t, k, j):
                    if L == 0:
                        hold(pool, s_win[k], 32 * (j + 1), s_tick)
                    hold(pool, s_desc, (t + L * T - 1) * CH, s_tick)
                    pool.tensor_copy(idx[:, k, :], wsrc[:, bass.ds(t * CH, CH)]).then_inc(s_idx, 1)
                    hold(pool, s_idx, t + L * T + 1, s_tick)
                    for c in range(CH):
                        if c in SPLIT:
                            hold(pool, s_low, (t + L * T - 1) * NS + SPLIT.index(c) + 1, s_tick)
                        else:
                            hold(pool, s_used, (t + L * T - 1) * CH + c + 1, s_tick)
                        pool.indirect_dma_start(rows[:, c, :], None, table[L],
                                                bass.IndirectOffsetOnAxis(ap=idx[:, k, c:c + 1], axis=0),
                                                engine_sem=s_desc).then_inc(s_row[c], 16)

                tile(0, 0, 0)
                tile(1, 1, 0)
                with pool.Fori(1, NT // 2) as i:
                    tile(2 * i, 0, i)
                    tile(2 * i + 1, 1, i)

        @block.tensor
        def _(pe):
            pe.wait_ge(s_const, 16)
            pe.wait_ge(s_before, 1)
            pe.matmul(psT[:, 0, 0:1], before[:, :], ones[0:125, 0:1], start=True, stop=True).then_inc(s_pcount, 1)
            pe.wait_ge(s_startc, 1)
            pe.matmul(psA[0:1, 0, 0:128], startc[:, :], ident, start=True, stop=True).then_inc(s_pstart, 1)
            pe.wait_ge(s_falls, 1)
            pe.matmul(psT[0:1, 0, 0:1], falls[:, :], ones[0:125, 0:1], start=True, stop=True).then_inc(s_pfalls, 1)
            pe.wait_ge(s_flagr, 1)
            pe.matmul(psX[:, 0, 0:1], ones[0:1, :], flags[:, 2:3], start=True, stop=True).then_inc(s_pflag, 1)
            pe.wait_ge(s_flag, 1)
            flag = pe.value_load(flagi[0:1, 0:1], min_val=0, max_val=1)
            pe.wait_ge(s_w, 16)
            pe.wait_ge(s_base, 1)
            for L in range(2):
                with pe.If(flag):
                    with pe.Fori(0, GT) as g:
                        n = g + L * GT
                        pe.wait_ge(s_gf, n + 1)
                        pe.matmul(psT[0:125, 0, 0:125], gf[:, 0:1].to_broadcast([125, 125]), ident[0:125, 0:125],
                                  start=True, stop=True).then_inc(s_gd, 1)
                        pe.wait_ge(s_same, n + 1)
                        pe.wait_ge(s_gr, 32 * (n + 1))
                        pe.matmul(psX[0:125, 0, 0:2], same[:, :], grow[:, D:DX], start=True, stop=True)
                        pe.matmul(psA[0:125, 0, :], same[:, :], grow[:, 0:D], start=True, stop=True).then_inc(s_gs, 1)

                def visit(t, k, c):
                    n = t + L * T
                    if c == 0:
                        wait(pe, s_agg, n - 1)
                        if L == 0:
                            wait(pe, s_cnt, n - 1)
                    pe.wait_ge(s_hot, n * CH + c + 1)
                    if c in SPLIT:
                        pe.wait_ge(s_low, n * NS + SPLIT.index(c) + 1)
                    else:
                        pe.wait_ge(s_row[c], 16 * (n + 1))
                    first, last = c == 0, c == CH - 1
                    if L == 0:
                        pe.matmul(psC[0:PN, k, 0:2], hot[:, c, 0:PN], ones2[:, :], start=first, stop=last)
                    if last:
                        with pe.If(flag):
                            pe.wait_ge(s_ext, 16 * (n + 1))
                            if L == 0:
                                pe.matmul(psC[0:PN, k, 0:2], ident[0:PN, 0:PN], ext[:, D:DX],
                                          start=False, stop=False, skip_group_check=True)
                            pe.matmul(psA[0:PN, k, :], ident[0:PN, 0:PN], ext[:, 0:D], start=False, stop=False,
                                      skip_group_check=True).then_inc(s_extu, 1)
                    if c in SPLIT:
                        b = SPLIT.index(c) % PARTS
                        pe.matmul(psA[0:PN, k, :], hot[:, c, 0:PN], high[:, b, :], start=first, stop=False)
                        pe.matmul(psA[0:PN, k, :], hot[:, c, 0:PN], low[:, b, :], start=False,
                                  stop=last).then_inc(s_used, 1)
                    else:
                        pe.matmul(psA[0:PN, k, :], hot[:, c, 0:PN].bitcast(F32), rows[:, c, :], start=first,
                                  stop=last).then_inc(s_used, 1)

                def product(n, k, source, s, q):
                    m = pe.matmul(psH[0:PN, k, :], source[:, k, q, 0:PN], w[:, L, s, q, :],
                                  start=(s == 0 and q == 0), stop=(s == 1 and q == KC - 1))
                    if s == 1 and q == KC - 1:
                        m.then_inc(s_h, 1)

                def dense_step(t, k, j, c):
                    n = t + L * T
                    if c == 0:
                        pe.wait_ge(s_xs[k], 16 * (j + 1) if L == 0 else 16 * (NT // 2) + 32 * (j + 1))
                        wait(pe, s_xT, n)
                        for q in range(KC):
                            m = pe.transpose(psX[:, q, 0:PN], xs[0:PN, k, q * 128:(q + 1) * 128], ident[0:PN, 0:PN])
                        m.then_inc(s_xt, 1)
                    if c == 5:
                        pe.wait_ge(s_agg, n + 1)
                        wait(pe, s_aT, n)
                        for q in range(KC):
                            m = pe.transpose(psT[:, q, 0:PN], agg[0:PN, k, q * 128:(q + 1) * 128], ident[0:PN, 0:PN])
                        m.then_inc(s_at, 1)
                    if 6 <= c < 6 + KC:
                        if c == 6:
                            pe.wait_ge(s_xT, n + 1)
                            wait(pe, s_hb, n - 1)
                        product(n, k, xT, 0, c - 6)
                    if 6 + KC <= c < 6 + 2 * KC:
                        if c == 6 + KC:
                            pe.wait_ge(s_aT, n + 1)
                        product(n, k, aT, 1, c - 6 - KC)

                def period(t, k, j, jp, chunks, dense, norms):
                    for c in range(CH):
                        if chunks:
                            visit(t, k, c)
                        if dense:
                            dense_step(t - 1, 1 - k, jp, c)

                over_periods(pe, period)

        @block.scalar
        def _(act):
            act.wait_ge(s_const, 16)
            for L in range(2):
                def split(t, k, c):
                    n, i = t + L * T, SPLIT.index(c)
                    act.wait_ge(s_row[c], 16 * (n + 1))
                    wait(act, s_used, last_in_slot(n, i))
                    act.activation(high[:, i % PARTS, :], rows[:, c, :], ACT.Copy).then_inc(s_high, 1)

                def dense_step(t, k, c):
                    n = t + L * T
                    if c == 3:
                        act.wait_ge(s_xt, n + 1)
                        act.activation(xT[:, k, :, 0:PN], psX[:, :, 0:PN], ACT.Copy).then_inc(s_xT, 1)
                    if c == 4:
                        act.wait_ge(s_used, CH * (n + 1))
                        act.wait_ge(s_rc, n + 1)
                        act.activation(agg[0:PN, k, :], psA[0:PN, k, :], ACT.Copy,
                                       scale=rcnt[0:PN, k:k + 1]).then_inc(s_agg, 1)
                    if c == 8:
                        act.wait_ge(s_at, n + 1)
                        act.activation(aT[:, k, :, 0:PN], psT[:, :, 0:PN], ACT.Copy).then_inc(s_aT, 1)

                def norm_step(t, c):
                    n = t + L * T
                    eps = cst[0:PN, C_EPS:C_EPS + 1]
                    if c == 4 and L == 0:
                        act.wait_ge(s_mv, n + 1)
                        act.activation(sd[0:PN, 0:1], mv[0:PN, 0, 1:2], ACT.Sqrt, bias=eps).then_inc(s_sd, 1)
                    if c == 10:
                        act.wait_ge(s_mv2, n + 1)
                        act.activation(sd[0:PN, 1:2], mv[0:PN, 1, 1:2], ACT.Sqrt, bias=eps).then_inc(s_sd2, 1)
                    if c == 12 and L == 0:
                        act.wait_ge(s_v1, n + 1)
                        act.activation(sd[0:PN, 2:3], rstd[0:PN, 2:3], ACT.Sqrt, bias=eps).then_inc(s_sd3, 1)

                def period(t, k, j, jp, chunks, dense, norms):
                    for c in range(CH):
                        if chunks and c in SPLIT:
                            split(t, k, c)
                        if dense:
                            dense_step(t - 1, 1 - k, c)
                        if norms:
                            norm_step(t - 2, c)

                over_periods(act, period)

        @block.vector
        def _(v):
            linked = [0]

            def link(ins):
                linked[0] += 1
                ins.then_inc(s_link, 1)
                v.wait_ge(s_link, linked[0])

            link(v.memset(grow[:, D:DX], 1.0))
            v.wait_ge(s_const, 16)
            link(v.tensor_copy(ones2[:, :], ones[:, 0:2]))
            v.wait_ge(s_dall, 32)
            link(v.tensor_copy(dallf[:, :], dall[:, :]))
            v.tensor_scalar(before[:, :], cst[0:125, C_THR:C_THR + 128], dallf[:, ER - 1:ER], None,
                            ALU.is_gt).then_inc(s_before, 1)
            v.wait_ge(s_pcount, 1)
            link(v.tensor_scalar(rowf[:, :], psT[:, 0, 0:1], 124.0, None, ALU.min))
            v.tensor_copy(rowi[:, :], rowf[:, :]).then_inc(s_rowi, 1)
            v.wait_ge(s_drow, 16)
            link(v.tensor_copy(drowf[:, :], drow[:, :]))
            link(v.tensor_scalar(drowl[:, :], drowf[:, :], cst[:, C_THRC:C_THRC + 1], None, ALU.is_lt))
            link(v.tensor_reduce(below[:, :], drowl[:, :], AX_X, ALU.add))
            v.scalar_tensor_tensor(out=startc[:, :], in0=rowf[:, :], scalar=float(ER), in1=below[:, :],
                                   op0=ALU.mult, op1=ALU.add).then_inc(s_startc, 1)
            link(v.tensor_tensor(drowf[0:125, :], dallf[:, 0:ER], dallf[:, 1:ER + 1], ALU.is_gt))
            v.tensor_reduce(falls[:, :], drowf[0:125, :], AX_X, ALU.add).then_inc(s_falls, 1)
            v.wait_ge(s_pstart, 1)
            link(v.tensor_scalar(startr[:, :], psA[0:1, 0, 0:NT], float(E - CAP), None, ALU.min))
            link(v.memset(starti[:, :], 0))
            link(v.tensor_copy(starti[:, 0:NT], startr[:, :]))
            link(v.tensor_tensor(length[:, :], psA[0:1, 0, HI:HI + NT], startr[:, :], ALU.subtract))
            link(v.tensor_reduce(longest[:, :], length[:, :], AX_X, ALU.max))
            v.wait_ge(s_pfalls, 1)
            link(v.tensor_scalar(flags[:, 0:1], psT[0:1, 0, 0:1], 0.5, None, ALU.is_gt))
            link(v.tensor_scalar(flags[:, 1:2], longest[:, :], CAP + 0.5, None, ALU.is_gt))
            v.tensor_tensor(flags[:, 2:3], flags[:, 0:1], flags[:, 1:2], ALU.max).then_inc(s_flagr, 1)
            v.wait_ge(s_flagr, 1)
            v.tensor_copy(flagi[:, :], flags[:, 2:3]).then_inc(s_flag, 1)
            v.wait_ge(s_pflag, 1)
            link(v.tensor_scalar(far[:, :], psX[:, 0, 0:1], FAR, None, ALU.mult))
            v.tensor_scalar(base[:, :], cst[:, C_BASE:C_BASE + NT], far[:, 0:1], None, ALU.add).then_inc(s_base, 1)
            v.wait_ge(s_base, 1)
            v.wait_ge(s_flag, 1)
            flag = v.value_load(flagi[0:1, 0:1], min_val=0, max_val=1)
            v.wait_ge(s_vec, 16)

            def general(L):
                v.memset(ext[:, :], 0.0).then_inc(s_extz, 1)
                with v.Fori(0, GT) as g:
                    n = g + L * GT
                    v.wait_ge(s_gi, 32 * (n + 1))
                    v.tensor_copy(gf[:, :], gi[:, 1:2]).then_inc(s_gf, 1)
                    v.wait_ge(s_gd, n + 1)
                    v.tensor_scalar(same[:, :], psT[0:125, 0, 0:125], gf[:, 0:1], None, ALU.is_equal).then_inc(s_same, 1)
                    v.wait_ge(s_same, n + 1)
                    v.tensor_tensor(mask[:, :], same[:, :], cst[0:125, C_TRI:C_TRI + 125], ALU.mult).then_inc(s_gstep, 1)
                    v.wait_ge(s_gstep, 5 * n + 1)
                    v.tensor_reduce(rank[:, 0:1], mask[:, :], AX_X, ALU.max).then_inc(s_gstep, 1)
                    v.tensor_tensor(rank[:, 1:2], cst[0:125, C_DUMP:C_DUMP + 1], gf[:, :], ALU.subtract).then_inc(s_gstep, 1)
                    v.wait_ge(s_gstep, 5 * n + 3)
                    v.tensor_tensor(rank[:, 2:3], rank[:, 0:1], rank[:, 1:2], ALU.mult).then_inc(s_gstep, 1)
                    v.wait_ge(s_gstep, 5 * n + 4)
                    v.tensor_tensor(gto[:, :], rank[:, 2:3], gf[:, :], ALU.add).then_inc(s_gto, 1)
                    v.wait_ge(s_gs, n + 1)
                    v.tensor_tensor(gold[:, D:DX], gold[:, D:DX], psX[0:125, 0, 0:2], ALU.add).then_inc(s_gstep, 1)
                    v.wait_ge(s_gstep, 5 * n + 5)
                    v.tensor_tensor(gold[:, 0:D], gold[:, 0:D], psA[0:125, 0, :], ALU.add).then_inc(s_gnew, 1)

            for L in range(2):
                if L == 1:
                    v.wait_ge(s_used, CH * NT)
                with v.If(flag):
                    if L == 1:
                        v.wait_ge(s_extu, NT)
                    general(L)

                def keys(t, k, j):
                    n = t + L * T
                    if L == 0:
                        v.wait_ge(s_win[k], 32 * (j + 1))
                    wait(v, s_hot, (n - 1) * CH)
                    v.tensor_tensor(key[:, k, :], wdst[:, bass.ds(t * CH, CH)],
                                    base[:, bass.ds(t, 1)].to_broadcast([128, CH]), ALU.subtract).then_inc(s_key, 1)
                    v.wait_ge(s_key, n + 1)

                def one_hot(t, k, c):
                    n = t + L * T
                    wait(v, s_used, (n - 1) * CH + c + 1)
                    v.tensor_scalar(hot[:, c, :], iota, key[:, k, c:c + 1], None, ALU.is_equal).then_inc(s_hot, 1)

                def moments(b, src_sb, s_in, s_stats, s_mvs, n):
                    v.wait_ge(s_in, n + 1)
                    v.bn_stats(st[0:PN, b, :], src_sb).then_inc(s_stats, 1)
                    hold(v, s_stats, n + 1, s_tick)
                    v.bn_aggr(mv[0:PN, b, :], st[0:PN, b, :]).then_inc(s_mvs, 1)

                def inverse(b, s_dev, s_out, n):
                    v.wait_ge(s_dev, n + 1)
                    r = (0, 1, 3)[b]
                    v.reciprocal(rstd[0:PN, r:r + 1], sd[0:PN, b:b + 1]).then_inc(s_out, 1)
                    v.wait_ge(s_out, n + 1)

                def split(t, k, c):
                    n, i = t + L * T, SPLIT.index(c)
                    v.wait_ge(s_high, n * NS + i + 1)
                    v.tensor_tensor(low[:, i % PARTS, :], rows[:, c, :], high[:, i % PARTS, :].bitcast(F32),
                                    ALU.subtract).then_inc(s_low, 1)

                def dense_step(t, k, c):
                    n = t + L * T
                    if c == 3:
                        wait(v, s_agg, n - 1)
                        if L == 0:
                            v.wait_ge(s_used, CH * (n + 1))
                            v.tensor_scalar(cntm[0:PN, k:k + 1], psC[0:PN, k, 0:1], 1.0, None, ALU.max).then_inc(s_cnt, 1)
                            v.wait_ge(s_cnt, n + 1)
                            v.reciprocal(rcnt[0:PN, k:k + 1], cntm[0:PN, k:k + 1]).then_inc(s_rc, 1)
                            v.wait_ge(s_rc, n + 1)
                            v.tensor_scalar(rcall[0:PN, bass.ds(t, 1)], rcnt[0:PN, k:k + 1], 1.0, None,
                                            ALU.mult).then_inc(s_rca, 1)
                        else:
                            v.wait_ge(s_rca, NT)
                            v.tensor_scalar(rcnt[0:PN, k:k + 1], rcall[0:PN, bass.ds(t, 1)], 1.0, None,
                                            ALU.mult).then_inc(s_rc, 1)

                def norm_step(t, k, j, c):
                    n = t + L * T
                    mv0, mv1 = mv[0:PN, 0, :], mv[0:PN, 1, :]
                    if c == 1:
                        v.wait_ge(s_h, n + 1)
                        wait(v, s_hn if L == 0 else s_ha, n)
                        v.tensor_tensor(hb[0:PN, :], psH[0:PN, k, :], vec[0:PN, 0 if L == 0 else 5, :],
                                        ALU.add).then_inc(s_hb, 1)
                    if L == 0:
                        if c == 2:
                            moments(0, hb[0:PN, :], s_hb, s_st, s_mv, n)
                        if c == 4:
                            inverse(0, s_sd, s_rs, n)
                            v.tensor_scalar(hn[0:PN, :], hb[0:PN, :], mv0[:, 0:1], rstd[0:PN, 0:1],
                                            ALU.subtract, ALU.mult).then_inc(s_hn, 1)
                        if c == 5:
                            v.wait_ge(s_hn, n + 1)
                            v.tensor_tensor(hg[0:PN, :], hn[0:PN, :], vec[0:PN, 1, :], ALU.mult).then_inc(s_hg, 1)
                        if c == 6:
                            v.wait_ge(s_hg, n + 1)
                            v.tensor_tensor(ha[0:PN, :], hg[0:PN, :], vec[0:PN, 2, :], ALU.add).then_inc(s_ha, 1)
                        if c == 7:
                            v.wait_ge(s_ha, n + 1)
                            v.scalar_tensor_tensor(out=u[0:PN, :], in0=ha[0:PN, :], scalar=0.0, in1=xs[0:PN, k, :],
                                                   op0=ALU.max, op1=ALU.add).then_inc(s_u, 1)
                    else:
                        if c == 3:
                            v.wait_ge(s_hb, n + 1)
                            v.wait_ge(s_xs[k], 16 * (NT // 2) + 32 * (j + 1))
                            v.scalar_tensor_tensor(out=ha[0:PN, :], in0=hb[0:PN, :], scalar=0.0, in1=xr[0:PN, k, :],
                                                   op0=ALU.max, op1=ALU.add).then_inc(s_ha, 1)
                        if c == 5:
                            v.wait_ge(s_ha, n + 1)
                            v.tensor_tensor(u[0:PN, :], ha[0:PN, :], xr[0:PN, k, :], ALU.add).then_inc(s_u, 1)
                    if c == 8:
                        moments(1, u[0:PN, :], s_u, s_st2, s_mv2, n)
                    if c == 10:
                        inverse(1, s_sd2, s_rs2, n)
                        if L == 0:
                            v.tensor_scalar(rstd[0:PN, 2:3], mv1[:, 1:2], rstd[0:PN, 1:2], rstd[0:PN, 1:2],
                                            ALU.mult, ALU.mult).then_inc(s_v1, 1)
                        wait(v, s_stx[k], 16 * (j + L * (NT // 2)))
                        v.tensor_scalar(x1o[0:PN, k, :], u[0:PN, :], mv1[:, 0:1], rstd[0:PN, 1:2],
                                        ALU.subtract, ALU.mult).then_inc(s_x1, 1)
                    if c == 12 and L == 0:
                        v.wait_ge(s_x1, n + 1)
                        inverse(2, s_sd3, s_rs3, n)
                        v.scalar_tensor_tensor(out=hs[0:PN, :], in0=x1o[0:PN, k, :], scalar=rstd[0:PN, 3:4],
                                               in1=vec[0:PN, 3, :], op0=ALU.mult, op1=ALU.mult).then_inc(s_hs, 1)
                    if c == 13 and L == 0:
                        v.wait_ge(s_hs, n + 1)
                        wait(v, s_sth[k], 16 * j)
                        v.tensor_tensor(h1o[0:PN, k, :], hs[0:PN, :], vec[0:PN, 4, :], ALU.add).then_inc(s_h1, 1)

                def period(t, k, j, jp, chunks, dense, norms):
                    if chunks:
                        keys(t, k, j)
                    for c in range(CH):
                        if chunks:
                            one_hot(t, k, c)
                            if c in SPLIT:
                                split(t, k, c)
                        if dense:
                            dense_step(t - 1, 1 - k, c)
                        if norms:
                            norm_step(t - 2, k, j - 1, c)

                over_periods(v, period)


def kernel(x, src, dst, L0_gnn_w_self, L0_gnn_w_neigh, L0_gnn_bias, L0_gnn_gamma, L0_gnn_beta,
           L1_gnn_W_l, L1_gnn_b_l, L1_gnn_W_r, L1_gnn_gamma, L1_gnn_beta):
    import numpy as np
    import concourse.bacc as bacc
    from concourse.bass_utils import run_bass_kernel_spmd

    w = np.stack([np.asarray(a) for a in (L0_gnn_w_self, L0_gnn_w_neigh, L1_gnn_W_r, L1_gnn_W_l)])
    w = w.reshape(2, 2, D, KC, 128).transpose(4, 0, 1, 3, 2)
    vecs = np.stack([np.asarray(a) for a in (L0_gnn_bias, L0_gnn_gamma, L0_gnn_beta, L1_gnn_gamma, L1_gnn_beta,
                                             L1_gnn_b_l)])
    arrays = {
        "x": np.ascontiguousarray(x), "src": np.ascontiguousarray(src), "dst": np.ascontiguousarray(dst),
        "wT": np.ascontiguousarray(w.reshape(128, 4 * KC * D)),
        "vecs": np.ascontiguousarray(np.broadcast_to(vecs.reshape(1, 6 * D), (128, 6 * D))),
        "consts": constants(np),
    }
    nc = bacc.Bacc("TRN2", target_bir_lowering=False, num_devices=1)
    ins = [nc.dram_tensor(n, a.shape, mybir.dt.from_np(a.dtype), kind="ExternalInput").ap() for n, a in arrays.items()]
    out = nc.dram_tensor("out", (N, D), F32, kind="ExternalOutput").ap()
    h1 = nc.dram_tensor("h1", (N, D), F32, kind="Internal").ap()
    x1 = nc.dram_tensor("x1", (N, D), F32, kind="Internal").ap()
    sums = nc.dram_tensor("sums", (N + PN, DX), F32, kind="Internal").ap()
    build(nc, *ins, out, h1, x1, sums)
    r = run_bass_kernel_spmd(nc, [arrays], core_ids=[0])
    return r.results[0]["out"]
```

```python
from contextlib import ExitStack

import concourse.bass as bass
from concourse import mybir

F32 = mybir.dt.float32
F32R = mybir.dt.float32r
I32 = mybir.dt.int32
ALU = mybir.AluOpType
ACT = mybir.ActivationFunctionType
AX_X = mybir.AxisListType.X

N, E, D = 6250, 100000, 512
EPS = 1e-5
PN = 125
NT = N // PN
MAIN = 16
TAIL = MAIN
CH = MAIN + 1
CAP = CH * 128
GROUP = 4
GROUPS = MAIN // GROUP
KC = D // 128
WHOLE = (1, 4, TAIL)
SPLIT = tuple(c for c in range(CH) if c not in WHOLE)
NS = len(SPLIT)
PARTS = 8
ER = E // 125
GT = E // 125
HI = 64
FAR = 1.0e6
DX = D + 2

C_ID, C_IOTA, C_THR, C_TRI, C_ONE = 0, 128, 256, 384, 512
C_THRC, C_BASE, C_DUMP = 640, 641, 641 + NT
C_EPS = C_DUMP + 1
C_ALL = C_EPS + 1


def constants(np):
    c = np.zeros((128, C_ALL), np.float32)
    p = np.arange(128)
    c[:, C_ID:C_ID + 128] = np.eye(128)
    c[:, C_IOTA:C_IOTA + 128] = p
    thr = np.where(p < HI, PN * p, PN * (p - HI + 1))
    c[:, C_THR:C_THR + 128] = thr
    c[:, C_TRI:C_TRI + 128] = p[None, :] < p[:, None]
    c[:, C_ONE:C_ONE + 128] = 1.0
    c[:, C_THRC] = thr
    c[:, C_BASE:C_BASE + NT] = PN * np.arange(NT)
    c[:, C_DUMP] = N + p
    c[:, C_EPS] = EPS
    return c


def wait(eng, sem, value):
    if not isinstance(value, int) or value > 0:
        eng.wait_ge(sem, value)


def hold(eng, sem, value, tick):
    wait(eng, sem, value)
    if not isinstance(value, int):
        eng.sem_inc(tick, 1)


C_OWNT, C_OWNC, C_OWN = 0, 5, 6
C_RC, C_MEAN, C_MEANT, C_MEANC, C_MEANP = 5, 7, 9, 12, 12
C_RCP = C_RC + 1
C_RSTD0, C_RSTD1, C_SD1, C_RSTD = 6, 11, 14, 14
C_HB, C_HG, C_DEV0, C_HA, C_U, C_HS, C_DEV1, C_SHIFT, C_X1, C_H1 = 3, 4, 5, 7, 8, 9, 10, 12, 15, 15


def over_periods(eng, period):
    period(0, 0, 0, -1, True, False, False)
    period(1, 1, 0, 0, True, True, False)
    with eng.Fori(1, NT // 2) as i:
        period(2 * i, 0, i, i - 1, True, True, True)
        period(2 * i + 1, 1, i, i, True, True, True)
    period(NT, 0, NT // 2, NT // 2 - 1, False, True, True)
    period(NT + 1, 1, NT // 2, NT // 2, False, False, True)


def last_in_slot(n, i):
    if i >= PARTS:
        return n * MAIN + SPLIT[i - PARTS] + 1
    last = max(q for q in range(NS) if q % PARTS == i)
    return (n - 1) * MAIN + SPLIT[last] + 1


def build(nc, x, src, dst, wT, vecs, consts, out, h1, x1, sums):
    with ExitStack() as ctx:
        def sb(name, shape, dt=F32):
            return ctx.enter_context(nc.sbuf_tensor(name, shape, dt))

        def pb(name, shape, dt=F32):
            return ctx.enter_context(nc.psum_tensor(name, shape, dt))

        def sem(name):
            return ctx.enter_context(nc.semaphore(name))

        cst = sb("cst", [128, C_ALL])
        w = sb("w", [128, 2, 2, KC, D])
        vec = sb("vec", [128, 6, D])
        ident = cst[:, C_ID:C_ID + 128]
        iota = cst[:, C_IOTA:C_IOTA + 128]
        ones = cst[:, C_ONE:C_ONE + 128]
        rows = sb("rows", [128, CH, D])
        scratch = rows[:, :, :].rearrange("p c d -> p (c d)")
        dall = sb("dall", [125, ER + 1], I32)
        dallf = scratch[0:125, 0:ER + 1]
        before = sb("before", [125, 128])
        rowf = sb("rowf", [128, 1])
        rowi = sb("rowi", [128, 1], I32)
        warm = sb("warm", [PN, 1])
        drow = sb("drow", [128, ER], I32)
        fallf = scratch[0:125, 3072:3072 + ER]
        drowf, drowl = scratch[:, 1024:1024 + ER], scratch[:, 2048:2048 + ER]
        below = sb("below", [128, 1])
        far = sb("far", [128, 1])
        startc = sb("startc", [128, 1])
        falls = sb("falls", [125, 1])
        startr = sb("startr", [1, NT])
        starti = sb("starti", [1, NT + 2], I32)
        length = sb("length", [1, NT])
        tails = sb("tails", [1, NT], I32)
        tailf = sb("tailf", [1, 2, 2 * NT])
        landed = sb("landed", [1, 2 * NT], I32)
        longest = sb("longest", [1, 1])
        flags = sb("flags", [1, 3])
        flagi = sb("flagi", [1, 1], I32)
        base = sb("base", [128, NT])
        wsrc = sb("wsrc", [128, (NT + 2) * CH], I32)
        wdst = sb("wdst", [128, (NT + 2) * CH], I32)
        idx = sb("idx", [128, 2, CH], I32)
        key = sb("key", [128, 2, CH])
        hot = sb("hot", [128, CH, 128], F32R)
        high = sb("high", [128, PARTS, D], F32R)
        low = sb("low", [128, PARTS, D], F32R)
        ones2 = sb("ones2", [128, 2], F32R)
        xs = sb("xs", [128, 2, D])
        xr = sb("xr", [128, 2, D])
        xT = sb("xT", [128, 2, KC, 128])
        agg = sb("agg", [128, 2, D])
        aT = sb("aT", [128, 2, KC, 128])
        ext = sb("ext", [125, DX])
        cntm = sb("cntm", [128, 2])
        rcnt = sb("rcnt", [128, 2])
        rcall = sb("rcall", [128, NT])
        hb = sb("hb", [128, D])
        hg = sb("hg", [128, D])
        ha = sb("ha", [128, D])
        u = sb("u", [128, D])
        hs = sb("hs", [128, D])
        squares = sb("squares", [128, D])
        xr2 = sb("xr2", [128, 2, D])
        total = sb("total", [128, 2])
        nmean = sb("nmean", [128, 2])
        spread = sb("spread", [128, 2])
        sd = sb("sd", [128, 2])
        rstd = sb("rstd", [128, 2])
        shift = sb("shift", [128, 1])
        var1 = sb("var1", [128, 1])
        sd1 = sb("sd1", [128, 1])
        rstd1 = sb("rstd1", [128, 1])
        scale1 = sb("scale1", [128, 1])
        x1o = sb("x1o", [128, 2, D])
        h1o = sb("h1o", [128, 2, D])
        gi = sb("gi", [125, 2], I32)
        gf = sb("gf", [125, 1])
        grow = sb("grow", [125, DX])
        gold = sb("gold", [125, DX])
        same = sb("same", [125, 125])
        mask = sb("mask", [125, 125])
        rank = sb("rank", [125, 3])
        gto = sb("gto", [125, 1], I32)
        psA = pb("psA", [128, 2, D])
        psC = pb("psC", [128, 2, D])
        psX = pb("psX", [128, KC, 128])
        psT = pb("psT", [128, KC, 128])
        psH = pb("psH", [128, 2, D])

        s_const, s_vec, s_dall, s_w = sem("s_const"), sem("s_vec"), sem("s_dall"), [sem(f"s_w{L}") for L in range(2)]
        s_starti, s_landed, s_pad, s_drow, s_tick, s_link = sem("s_starti"), sem("s_landed"), sem("s_pad"), sem("s_drow"), sem("s_tick"), sem("s_link")
        s_before, s_rowi, s_startc, s_falls, s_flagr, s_flag = [sem("s_" + n) for n in ("before", "rowi", "startc", "falls", "flagr", "flag")]
        s_pcount, s_pstart, s_pfalls, s_pflag = [sem("s_p" + n) for n in ("count", "start", "falls", "flag")]
        s_win = [sem(f"s_win{k}") for k in range(2)]
        s_idx = sem("s_idx")
        s_desc = sem("s_desc")
        s_row = [sem(f"s_row{c}") for c in range(CH)]
        s_used = sem("s_used")
        s_high, s_low = sem("s_high"), sem("s_low")
        s_key, s_hot = sem("s_key"), sem("s_hot")
        s_xs = [sem(f"s_xs{k}") for k in range(2)]
        s_xt, s_xT = sem("s_xt"), sem("s_xT")
        s_cnt, s_rc, s_rca = sem("s_cnt"), sem("s_rc"), sem("s_rca")
        s_agg, s_at, s_aT = sem("s_agg"), sem("s_at"), sem("s_aT")
        s_ext, s_extu = sem("s_ext"), sem("s_extu")
        s_h = sem("s_h")
        s_hb, s_hg, s_ha, s_u, s_hs, s_x1, s_h1, s_xr2 = [sem("s_" + n) for n in ("hb", "hg", "ha", "u", "hs", "x1", "h1", "xr2")]
        s_nmean, s_spread, s_sd, s_rstd = [[sem(f"s_{n}_{b}") for b in range(2)] for n in ("nmean", "spread", "sd", "rstd")]
        s_shift, s_var1, s_sd1, s_rstd1, s_scale1 = [sem("s_" + n) for n in ("shift", "var1", "sd1", "rstd1", "scale1")]
        s_stx = [sem(f"s_stx{k}") for k in range(2)]
        s_sth = [sem(f"s_sth{k}") for k in range(2)]

        s_base, s_extz, s_zero, s_gi, s_gr, s_gf, s_gd, s_same, s_gs, s_gnew, s_gto, s_gout, s_gone = [
            sem("s_" + n) for n in ("base", "extz", "zero", "gi", "gr", "gf", "gd", "same", "gs", "gnew", "gto", "gout", "gone")]
        s_gstep = sem("s_gstep")

        block = ctx.enter_context(nc.Block())
        table = [x, h1]
        T = NT

        @block.sync
        def _(sp):
            sp.dma_start(cst[:, :], consts).then_inc(s_const, 16)
            sp.dma_start(dall[:, 0:ER], dst.rearrange("(p e) -> p e", p=125)).then_inc(s_dall, 16)
            sp.wait_ge(s_pad, 1)
            with nc.allow_non_contiguous_dma(reason="one column of the next row's first edges"):
                sp.dma_start(dall[0:124, ER:ER + 1],
                             dst.rearrange("(p e) -> p e", p=125)[1:125, 0:1]).then_inc(s_dall, 16)

            def load_window(t, k, j):
                hold(sp, s_win[k], 64 * j, s_tick)
                at = sp.value_load(starti[0:1, bass.ds(t, 1)], min_val=0, max_val=E - CAP)
                for column, edges in ((wsrc, src), (wdst, dst)):
                    sp.dma_start(column[:, bass.ds(t * CH, MAIN)],
                                 edges[bass.ds(at, MAIN * 128)].rearrange("(p c) -> p c", c=MAIN)).then_inc(s_win[k], 16)
                    sp.dma_start(column[:, bass.ds(t * CH + TAIL, 1)],
                                 edges[bass.ds(at + MAIN * 128, 128)].rearrange("(p c) -> p c", c=1)).then_inc(s_win[k], 16)

            sp.wait_ge(s_starti, 1)
            load_window(0, 0, 0)
            load_window(1, 1, 0)

            def load_weights(L):
                sp.wait_ge(s_used, 1 if L == 0 else MAIN + 1)
                sp.dma_start(w[:, L, :, :, :].rearrange("p s c d -> p (s c d)"),
                             wT[:, L * 2 * KC * D:(L + 1) * 2 * KC * D]).then_inc(s_w[L], 16)
                if L == 0:
                    sp.dma_start(vec[:, :, :], vecs.rearrange("p (v d) -> p v d", v=6)).then_inc(s_vec, 16)

            sp.wait_ge(s_flag, 1)
            flag = sp.value_load(flagi[0:1, 0:1], min_val=0, max_val=1)
            for L in range(2):
                def load_rows(t, k, j):
                    hold(sp, s_u, t + L * T - 1, s_tick)
                    hold(sp, s_xt, t + L * T - 1, s_tick)
                    sp.dma_start(xs[0:PN, k, :], table[L][bass.ds(t * PN, PN), :]).then_inc(s_xs[k], 16)
                    if L == 1:
                        sp.dma_start(xr[0:PN, k, :], x1[bass.ds(t * PN, PN), :]).then_inc(s_xs[k], 16)

                def tile(t, k, j):
                    if L == 0:
                        load_window(t + 2, k, j + 1)
                    load_rows(t, k, j)
                    with sp.If(flag):
                        hold(sp, s_extu, t + L * T, s_tick)
                        sp.dma_start(ext[:, :], sums[bass.ds(t * PN, PN), :]).then_inc(s_ext, 16)

                def store(t, k, j):
                    hold(sp, s_x1, t + L * T + 1, s_tick)
                    sp.dma_start((x1 if L == 0 else out)[bass.ds(t * PN, PN), :], x1o[0:PN, k, :]).then_inc(s_stx[k], 16)
                    if L == 0:
                        hold(sp, s_h1, t + 1, s_tick)
                        sp.dma_start(h1[bass.ds(t * PN, PN), :], h1o[0:PN, k, :]).then_inc(s_sth[k], 16)

                if L == 1:
                    for k in range(2):
                        sp.wait_ge(s_sth[k], 16 * (NT // 2))
                        sp.wait_ge(s_stx[k], 16 * (NT // 2))
                with sp.If(flag):
                    if L == 0:
                        sp.wait_ge(s_extz, 1)
                    else:
                        sp.wait_ge(s_ext, 16 * NT)
                        sp.wait_ge(s_extz, 2)
                    with sp.Fori(0, NT + 1) as i:
                        sp.dma_start(sums[bass.ds(i * PN, PN), :], ext[:, :]).then_inc(s_zero, 16)
                        hold(sp, s_zero, 16 * (i + 1 + L * (NT + 1)), s_tick)
                    with sp.Fori(0, GT) as g:
                        sp.dma_start(gi[:, 0:1], src[bass.ds(g * 125, 125)].rearrange("(p c) -> p c", c=1)).then_inc(s_gi, 16)
                        sp.dma_start(gi[:, 1:2], dst[bass.ds(g * 125, 125)].rearrange("(p c) -> p c", c=1)).then_inc(s_gi, 16)
                        hold(sp, s_gone, g + L * GT + 1, s_tick)
                tile(0, 0, 0)
                if L == 0:
                    load_weights(0)
                tile(1, 1, 0)
                if L == 0:
                    load_weights(1)
                with sp.Fori(1, NT // 2) as i:
                    tile(2 * i, 0, i)
                    store(2 * i - 2, 0, i - 1)
                    tile(2 * i + 1, 1, i)
                    store(2 * i - 1, 1, i - 1)
                store(NT - 2, 0, NT // 2 - 1)
                store(NT - 1, 1, NT // 2 - 1)
            for k in range(2):
                sp.wait_ge(s_stx[k], 16 * NT)
                sp.wait_ge(s_win[k], 64 * (NT // 2 + 1))

        @block.gpsimd
        def _(pool):
            pool.memset(dall[:, ER:ER + 1], 1 << 20).then_inc(s_pad, 1)
            hold(pool, s_rowi, 1, s_tick)
            pool.indirect_dma_start(drow[:, :], None, dst.rearrange("(p e) -> p e", p=125),
                                    bass.IndirectOffsetOnAxis(ap=rowi[:, 0:1], axis=0)).then_inc(s_drow, 16)
            hold(pool, s_flag, 1, s_tick)
            flag = pool.value_load(flagi[0:1, 0:1], min_val=0, max_val=1)
            for L in range(2):
                with pool.If(flag):
                    if L == 1:
                        for k in range(2):
                            hold(pool, s_sth[k], 16 * (NT // 2), s_tick)
                    hold(pool, s_zero, 16 * (NT + 1) * (L + 1), s_tick)
                    with pool.Fori(0, GT) as g:
                        n = g + L * GT
                        hold(pool, s_gi, 32 * (n + 1), s_tick)
                        pool.indirect_dma_start(grow[:, 0:D], None, table[L],
                                                bass.IndirectOffsetOnAxis(ap=gi[:, 0:1], axis=0)).then_inc(s_gr, 16)
                        pool.indirect_dma_start(gold[:, :], None, sums,
                                                bass.IndirectOffsetOnAxis(ap=gi[:, 1:2], axis=0)).then_inc(s_gr, 16)
                        hold(pool, s_gnew, n + 1, s_tick)
                        hold(pool, s_gto, n + 1, s_tick)
                        pool.indirect_dma_start(sums, bass.IndirectOffsetOnAxis(ap=gto[:, 0:1], axis=0),
                                                gold[:, :], None).then_inc(s_gout, 16)
                        hold(pool, s_gout, 16 * (n + 1), s_tick)
                        pool.sem_inc(s_gone, 1)

                def gather(k, c):
                    pool.indirect_dma_start(rows[:, c, :], None, table[L],
                                            bass.IndirectOffsetOnAxis(ap=idx[:, k, c:c + 1], axis=0),
                                            engine_sem=s_desc).then_inc(s_row[c], 16)

                def bring_indices(t, k, j):
                    if L == 0:
                        hold(pool, s_win[k], 64 * (j + 1), s_tick)
                    hold(pool, s_desc, (t + L * T - 1) * CH, s_tick)
                    pool.tensor_copy(idx[:, k, :], wsrc[:, bass.ds(t * CH, CH)]).then_inc(s_idx, 1)

                def tile(t, k, j):
                    hold(pool, s_idx, t + L * (T + 1) + 1, s_tick)
                    if L == 1 and isinstance(t, int) and t == 0:
                        for b in range(2):
                            hold(pool, s_sth[b], 16 * (NT // 2), s_tick)
                    hold(pool, s_landed, 1, s_tick)
                    tail = pool.value_load(tails[0:1, bass.ds(t, 1)], min_val=0, max_val=1)
                    for c in range(MAIN):
                        if c == MAIN - 1:
                            hold(pool, s_used, (t + L * T) * MAIN, s_tick)
                            with pool.If(tail):
                                gather(k, TAIL)
                            with pool.Else():
                                pool.sem_inc(s_desc, 1)
                        if c in SPLIT:
                            hold(pool, s_low, (t + L * T - 1) * NS + SPLIT.index(c) + 1, s_tick)
                        else:
                            hold(pool, s_used, (t + L * T - 1) * MAIN + c + 1, s_tick)
                        if c == MAIN - 1:
                            bring_indices(t + 1, 1 - k, j + k)
                        gather(k, c)

                if L == 1:
                    hold(pool, s_idx, T + 1, s_tick)
                bring_indices(0, 0, 0)
                tile(0, 0, 0)
                tile(1, 1, 0)
                with pool.Fori(1, NT // 2) as i:
                    tile(2 * i, 0, i)
                    tile(2 * i + 1, 1, i)

        @block.tensor
        def _(pe):
            pe.wait_ge(s_const, 16)
            pe.wait_ge(s_before, 1)
            pe.matmul(psT[:, 0, 0:1], before[:, :], ones[0:125, 0:1], start=True, stop=True).then_inc(s_pcount, 1)
            pe.wait_ge(s_falls, 1)
            pe.matmul(psT[0:1, 0, 0:1], falls[:, :], ones[0:125, 0:1], start=True, stop=True).then_inc(s_pfalls, 1)
            pe.wait_ge(s_startc, 1)
            pe.matmul(psA[0:1, 0, 0:128], startc[:, :], ident, start=True, stop=True).then_inc(s_pstart, 1)
            pe.wait_ge(s_flagr, 1)
            pe.matmul(psX[:, 0, 0:1], ones[0:1, :], flags[:, 2:3], start=True, stop=True).then_inc(s_pflag, 1)
            pe.wait_ge(s_flag, 1)
            flag = pe.value_load(flagi[0:1, 0:1], min_val=0, max_val=1)
            pe.wait_ge(s_base, 1)
            for L in range(2):
                with pe.If(flag):
                    with pe.Fori(0, GT) as g:
                        n = g + L * GT
                        pe.wait_ge(s_gf, n + 1)
                        pe.matmul(psT[0:125, 0, 0:125], gf[:, 0:1].to_broadcast([125, 125]), ident[0:125, 0:125],
                                  start=True, stop=True).then_inc(s_gd, 1)
                        pe.wait_ge(s_same, n + 1)
                        pe.wait_ge(s_gr, 32 * (n + 1))
                        pe.matmul(psX[0:125, 0, 0:2], same[:, :], grow[:, D:DX], start=True, stop=True)
                        pe.matmul(psA[0:125, 0, :], same[:, :], grow[:, 0:D], start=True, stop=True).then_inc(s_gs, 1)

                def visit(t, k, c):
                    n = t + L * T
                    if c == 0:
                        wait(pe, s_agg, n - 1)
                        if L == 0:
                            wait(pe, s_cnt, n - 1)
                    pe.wait_ge(s_hot, n * GROUPS + c // GROUP + 1)
                    if c in SPLIT:
                        pe.wait_ge(s_low, n * NS + SPLIT.index(c) + 1)
                    else:
                        pe.wait_ge(s_row[c], 16 * (n + 1))
                    first, last = c == 0, c == MAIN - 1
                    if last:
                        pe.wait_ge(s_landed, 1)
                        tail = pe.value_load(tails[0:1, bass.ds(t, 1)], min_val=0, max_val=1)
                        with pe.If(tail):
                            pe.wait_ge(s_row[TAIL], pe.value_load(landed[0:1, bass.ds(n, 1)], min_val=16, max_val=32 * NT))
                            if L == 0:
                                pe.matmul(psC[0:PN, k, 0:2], hot[:, TAIL, 0:PN], ones2[:, :], start=False, stop=False)
                            pe.matmul(psA[0:PN, k, :], hot[:, TAIL, 0:PN].bitcast(F32), rows[:, TAIL, :],
                                      start=False, stop=False)
                    if L == 0:
                        pe.matmul(psC[0:PN, k, 0:2], hot[:, c, 0:PN], ones2[:, :], start=first, stop=last)
                    if last:
                        with pe.If(flag):
                            pe.wait_ge(s_ext, 16 * (n + 1))
                            if L == 0:
                                pe.matmul(psC[0:PN, k, 0:2], ident[0:PN, 0:PN], ext[:, D:DX],
                                          start=False, stop=False, skip_group_check=True)
                            pe.matmul(psA[0:PN, k, :], ident[0:PN, 0:PN], ext[:, 0:D], start=False, stop=False,
                                      skip_group_check=True).then_inc(s_extu, 1)
                    if c in SPLIT:
                        b = SPLIT.index(c) % PARTS
                        pe.matmul(psA[0:PN, k, :], hot[:, c, 0:PN], high[:, b, :], start=first, stop=False)
                        pe.matmul(psA[0:PN, k, :], hot[:, c, 0:PN], low[:, b, :], start=False,
                                  stop=last).then_inc(s_used, 1)
                    else:
                        pe.matmul(psA[0:PN, k, :], hot[:, c, 0:PN].bitcast(F32), rows[:, c, :], start=first,
                                  stop=last).then_inc(s_used, 1)

                def product(n, k, source, s, q):
                    m = pe.matmul(psH[0:PN, k, :], source[:, k, q, 0:PN], w[:, L, s, q, :],
                                  start=(s == 0 and q == 0), stop=(s == 1 and q == KC - 1))
                    if s == 1 and q == KC - 1:
                        m.then_inc(s_h, 1)

                def dense_step(t, k, j, c):
                    n = t + L * T
                    if c == C_OWNT:
                        pe.wait_ge(s_xs[k], 16 * (j + 1) if L == 0 else 16 * (NT // 2) + 32 * (j + 1))
                        wait(pe, s_xT, n)
                        for q in range(KC):
                            m = pe.transpose(psX[:, q, 0:PN], xs[0:PN, k, q * 128:(q + 1) * 128], ident[0:PN, 0:PN])
                        m.then_inc(s_xt, 1)
                    if c == C_MEANT:
                        pe.wait_ge(s_agg, n + 1)
                        wait(pe, s_aT, n)
                        for q in range(KC):
                            m = pe.transpose(psT[:, q, 0:PN], agg[0:PN, k, q * 128:(q + 1) * 128], ident[0:PN, 0:PN])
                        m.then_inc(s_at, 1)
                    if C_OWN <= c < C_OWN + KC:
                        if c == C_OWN:
                            pe.wait_ge(s_w[L], 16)
                            pe.wait_ge(s_xT, n + 1)
                            wait(pe, s_hb if L == 0 else s_ha, n - 1)
                        product(n, k, xT, 0, c - C_OWN)
                    if C_MEANP <= c < C_MEANP + KC:
                        if c == C_MEANP:
                            pe.wait_ge(s_aT, n + 1)
                        product(n, k, aT, 1, c - C_MEANP)

                def period(t, k, j, jp, chunks, dense, norms):
                    for c in range(MAIN):
                        if chunks:
                            visit(t, k, c)
                        if dense:
                            dense_step(t - 1, 1 - k, jp, c)

                over_periods(pe, period)

        @block.scalar
        def _(act):
            act.wait_ge(s_const, 16)
            eps = cst[0:PN, C_EPS:C_EPS + 1]
            act.activation(warm[:, :], eps, ACT.Sqrt)
            for L in range(2):
                def split(t, k, c):
                    n, i = t + L * T, SPLIT.index(c)
                    act.wait_ge(s_row[c], 16 * (n + 1))
                    wait(act, s_used, last_in_slot(n, i))
                    act.activation(high[:, i % PARTS, :], rows[:, c, :], ACT.Copy).then_inc(s_high, 1)

                def dense_step(t, k, c):
                    n = t + L * T
                    if c == C_OWNC:
                        act.wait_ge(s_xt, n + 1)
                        act.activation(xT[:, k, :, 0:PN], psX[:, :, 0:PN], ACT.Copy).then_inc(s_xT, 1)
                    if c == C_MEAN:
                        act.wait_ge(s_used, MAIN * (n + 1))
                        act.wait_ge(s_rc, n + 1)
                        act.activation(agg[0:PN, k, :], psA[0:PN, k, :], ACT.Copy,
                                       scale=rcnt[0:PN, k:k + 1]).then_inc(s_agg, 1)
                        if L == 0:
                            act.activation(rcall[0:PN, bass.ds(t, 1)], rcnt[0:PN, k:k + 1], ACT.Copy).then_inc(s_rca, 1)
                    if c == C_MEANC:
                        act.wait_ge(s_at, n + 1)
                        act.activation(aT[:, k, :, 0:PN], psT[:, :, 0:PN], ACT.Copy).then_inc(s_aT, 1)

                def deviation(n, b, rows_sb):
                    act.wait_ge(s_nmean[b], n + 1)
                    act.activation(squares[0:PN, :], rows_sb, ACT.Square, bias=nmean[0:PN, b:b + 1],
                                   accum_out=spread[0:PN, b:b + 1]).then_inc(s_spread[b], 1)
                    act.wait_ge(s_spread[b], n + 1)
                    act.activation(sd[0:PN, b:b + 1], spread[0:PN, b:b + 1], ACT.Sqrt, bias=eps,
                                   scale=1.0 / D).then_inc(s_sd[b], 1)

                def norm_step(t, k, j, c):
                    n = t + L * T
                    if c == C_DEV0 and L == 0:
                        deviation(n, 0, hb[0:PN, :])
                    if c == 0 and L == 1:
                        act.wait_ge(s_xs[k], 16 * (NT // 2) + 32 * (j + 1))
                        wait(act, s_u, n - 1)
                        act.activation(xr2[0:PN, k, :], xr[0:PN, k, :], ACT.Copy, scale=2.0).then_inc(s_xr2, 1)
                    if c == C_DEV1:
                        deviation(n, 1, u[0:PN, :])
                    if c == C_SD1 and L == 0:
                        act.wait_ge(s_var1, n + 1)
                        act.activation(sd1[0:PN, :], var1[0:PN, :], ACT.Sqrt, bias=eps, scale=1.0 / D).then_inc(s_sd1, 1)
                    if c == C_X1:
                        act.wait_ge(s_shift, n + 1)
                        wait(act, s_stx[k], 16 * (j + L * (NT // 2)))
                        act.activation(x1o[0:PN, k, :], u[0:PN, :], ACT.Identity, bias=shift[0:PN, :],
                                       scale=rstd[0:PN, 1:2]).then_inc(s_x1, 1)

                def period(t, k, j, jp, chunks, dense, norms):
                    for c in range(MAIN):
                        if chunks and c in SPLIT:
                            split(t, k, c)
                        if dense:
                            dense_step(t - 1, 1 - k, c)
                        if norms and chunks:
                            norm_step(t - 2, k, j - 1, c)
                    for c in range(MAIN):
                        if norms and not chunks:
                            norm_step(t - 2, k, j - 1, c)

                over_periods(act, period)

        @block.vector
        def _(v):
            linked = [0]

            def link(ins):
                linked[0] += 1
                ins.then_inc(s_link, 1)
                v.wait_ge(s_link, linked[0])

            link(v.memset(grow[:, D:DX], 1.0))
            link(v.memset(starti[:, :], 0))
            v.wait_ge(s_const, 16)
            link(v.tensor_copy(ones2[:, :], ones[:, 0:2]))
            v.wait_ge(s_dall, 32)
            link(v.tensor_copy(dallf[:, :], dall[:, :]))
            v.tensor_scalar(before[:, :], cst[0:125, C_THR:C_THR + 128], dallf[:, ER - 1:ER], None,
                            ALU.is_gt).then_inc(s_before, 1)
            v.wait_ge(s_pcount, 1)
            link(v.tensor_scalar(rowf[:, :], psT[:, 0, 0:1], 124.0, None, ALU.min))
            v.tensor_copy(rowi[:, :], rowf[:, :]).then_inc(s_rowi, 1)
            link(v.tensor_tensor(fallf[:, :], dallf[:, 0:ER], dallf[:, 1:ER + 1], ALU.is_gt))
            v.tensor_reduce(falls[:, :], fallf[:, :], AX_X, ALU.add).then_inc(s_falls, 1)
            v.wait_ge(s_drow, 16)
            link(v.tensor_copy(drowf[:, :], drow[:, :]))
            link(v.tensor_scalar(drowl[:, :], drowf[:, :], cst[:, C_THRC:C_THRC + 1], None, ALU.is_lt))
            link(v.tensor_reduce(below[:, :], drowl[:, :], AX_X, ALU.add))
            v.scalar_tensor_tensor(out=startc[:, :], in0=rowf[:, :], scalar=float(ER), in1=below[:, :],
                                   op0=ALU.mult, op1=ALU.add).then_inc(s_startc, 1)
            v.wait_ge(s_pstart, 1)
            link(v.tensor_scalar(startr[:, :], psA[0:1, 0, 0:NT], float(E - CAP), None, ALU.min))
            v.tensor_copy(starti[:, 0:NT], startr[:, :]).then_inc(s_starti, 1)
            link(v.tensor_tensor(length[:, :], psA[0:1, 0, HI:HI + NT], startr[:, :], ALU.subtract))
            link(v.tensor_scalar(tails[:, :], length[:, :], MAIN * 128 + 0.5, None, ALU.is_gt))
            link(v.tensor_reduce(longest[:, :], length[:, :], AX_X, ALU.max))
            v.wait_ge(s_pfalls, 1)
            link(v.tensor_scalar(flags[:, 0:1], psT[0:1, 0, 0:1], 0.5, None, ALU.is_gt))
            link(v.tensor_scalar(flags[:, 1:2], longest[:, :], CAP + 0.5, None, ALU.is_gt))
            v.tensor_tensor(flags[:, 2:3], flags[:, 0:1], flags[:, 1:2], ALU.max).then_inc(s_flagr, 1)
            v.wait_ge(s_flagr, 1)
            v.tensor_copy(flagi[:, :], flags[:, 2:3]).then_inc(s_flag, 1)
            v.wait_ge(s_pflag, 1)
            link(v.tensor_scalar(far[:, :], psX[:, 0, 0:1], FAR, None, ALU.mult))
            v.tensor_scalar(base[:, :], cst[:, C_BASE:C_BASE + NT], far[:, 0:1], None, ALU.add).then_inc(s_base, 1)
            for L in range(2):
                link(v.tensor_scalar(tailf[:, 0, L * NT:(L + 1) * NT], tails[:, :], 16.0, None, ALU.mult))
            span, b = 1, 0
            while span < 2 * NT:
                link(v.tensor_copy(tailf[:, 1 - b, 0:span], tailf[:, b, 0:span]))
                link(v.tensor_tensor(tailf[:, 1 - b, span:], tailf[:, b, span:], tailf[:, b, 0:2 * NT - span], ALU.add))
                span, b = 2 * span, 1 - b
            v.tensor_copy(landed[:, :], tailf[:, b, :]).then_inc(s_landed, 1)
            v.wait_ge(s_base, 1)
            v.wait_ge(s_flag, 1)
            flag = v.value_load(flagi[0:1, 0:1], min_val=0, max_val=1)

            def general(L):
                v.memset(ext[:, :], 0.0).then_inc(s_extz, 1)
                with v.Fori(0, GT) as g:
                    n = g + L * GT
                    v.wait_ge(s_gi, 32 * (n + 1))
                    v.tensor_copy(gf[:, :], gi[:, 1:2]).then_inc(s_gf, 1)
                    v.wait_ge(s_gd, n + 1)
                    v.tensor_scalar(same[:, :], psT[0:125, 0, 0:125], gf[:, 0:1], None, ALU.is_equal).then_inc(s_same, 1)
                    v.wait_ge(s_same, n + 1)
                    v.tensor_tensor(mask[:, :], same[:, :], cst[0:125, C_TRI:C_TRI + 125], ALU.mult).then_inc(s_gstep, 1)
                    v.wait_ge(s_gstep, 5 * n + 1)
                    v.tensor_reduce(rank[:, 0:1], mask[:, :], AX_X, ALU.max).then_inc(s_gstep, 1)
                    v.tensor_tensor(rank[:, 1:2], cst[0:125, C_DUMP:C_DUMP + 1], gf[:, :], ALU.subtract).then_inc(s_gstep, 1)
                    v.wait_ge(s_gstep, 5 * n + 3)
                    v.tensor_tensor(rank[:, 2:3], rank[:, 0:1], rank[:, 1:2], ALU.mult).then_inc(s_gstep, 1)
                    v.wait_ge(s_gstep, 5 * n + 4)
                    v.tensor_tensor(gto[:, :], rank[:, 2:3], gf[:, :], ALU.add).then_inc(s_gto, 1)
                    v.wait_ge(s_gs, n + 1)
                    v.tensor_tensor(gold[:, D:DX], gold[:, D:DX], psX[0:125, 0, 0:2], ALU.add).then_inc(s_gstep, 1)
                    v.wait_ge(s_gstep, 5 * n + 5)
                    v.tensor_tensor(gold[:, 0:D], gold[:, 0:D], psA[0:125, 0, :], ALU.add).then_inc(s_gnew, 1)

            for L in range(2):
                if L == 1:
                    v.wait_ge(s_used, MAIN * NT)
                with v.If(flag):
                    if L == 1:
                        v.wait_ge(s_extu, NT)
                    general(L)

                def keys(t, k, j):
                    n = t + L * T
                    if L == 0:
                        v.wait_ge(s_win[k], 64 * (j + 1))
                    wait(v, s_hot, (n - 1) * GROUPS)
                    v.tensor_tensor(key[:, k, :], wdst[:, bass.ds(t * CH, CH)],
                                    base[:, bass.ds(t, 1)].to_broadcast([128, CH]), ALU.subtract).then_inc(s_key, 1)
                    v.wait_ge(s_key, n + 1)

                def one_hots(t, k, g):
                    n = t + L * T
                    first, end = g * GROUP, CH if g == GROUPS - 1 else (g + 1) * GROUP
                    wait(v, s_used, (n - 1) * MAIN + (g + 1) * GROUP)
                    shape = [128, end - first, 128]
                    v.tensor_tensor(hot[:, first:end, :], cst[:, None, C_IOTA:C_IOTA + 128].to_broadcast(shape),
                                    key[:, k, first:end, None].to_broadcast(shape), ALU.is_equal).then_inc(s_hot, 1)

                def minus_mean(n, b, s_in):
                    v.wait_ge(s_in, n + 1)
                    wait(v, s_sd[b], n)
                    v.tensor_scalar(nmean[0:PN, b:b + 1], total[0:PN, b:b + 1], -1.0 / D, None,
                                    ALU.mult).then_inc(s_nmean[b], 1)

                def inverse(n, b):
                    v.wait_ge(s_sd[b], n + 1)
                    v.reciprocal(rstd[0:PN, b:b + 1], sd[0:PN, b:b + 1]).then_inc(s_rstd[b], 1)

                def split(t, k, c):
                    n, i = t + L * T, SPLIT.index(c)
                    v.wait_ge(s_high, n * NS + i + 1)
                    v.tensor_tensor(low[:, i % PARTS, :], rows[:, c, :], high[:, i % PARTS, :].bitcast(F32),
                                    ALU.subtract).then_inc(s_low, 1)

                def dense_step(t, k, c):
                    n = t + L * T
                    if c == C_RC:
                        wait(v, s_agg, n - 1)
                        wait(v, s_rca, min(n - 1, T) if isinstance(n, int) else n - 1 if L == 0 else T)
                        if L == 0:
                            v.wait_ge(s_used, MAIN * (n + 1))
                            v.tensor_scalar(cntm[0:PN, k:k + 1], psC[0:PN, k, 0:1], 1.0, None, ALU.max).then_inc(s_cnt, 1)
                        else:
                            v.wait_ge(s_rca, NT)
                            v.tensor_scalar(rcnt[0:PN, k:k + 1], rcall[0:PN, bass.ds(t, 1)], 1.0, None,
                                            ALU.mult).then_inc(s_rc, 1)
                    if c == C_RCP and L == 0:
                        v.wait_ge(s_cnt, n + 1)
                        v.reciprocal(rcnt[0:PN, k:k + 1], cntm[0:PN, k:k + 1]).then_inc(s_rc, 1)

                def norm_step(t, k, j, c):
                    n = t + L * T
                    if L == 0:
                        if c == C_HB:
                            v.wait_ge(s_vec, 16)
                            v.wait_ge(s_h, n + 1)
                            wait(v, s_hg, n)
                            hold(v, s_sd[0], n, s_tick)
                            v.tensor_tensor_reduce(hb[0:PN, :], psH[0:PN, k, :], vec[0:PN, 0, :], 1.0, 0.0,
                                                   ALU.add, ALU.add, total[0:PN, 0:1]).then_inc(s_hb, 1)
                            minus_mean(n, 0, s_hb)
                        if c == C_HG:
                            v.wait_ge(s_nmean[0], n + 1)
                            v.scalar_tensor_tensor(out=hg[0:PN, :], in0=hb[0:PN, :], scalar=nmean[0:PN, 0:1],
                                                   in1=vec[0:PN, 1, :], op0=ALU.add, op1=ALU.mult).then_inc(s_hg, 1)
                        if c == C_RSTD0:
                            inverse(n, 0)
                        if c == C_HA:
                            v.wait_ge(s_rstd[0], n + 1)
                            v.wait_ge(s_hg, n + 1)
                            v.scalar_tensor_tensor(out=ha[0:PN, :], in0=hg[0:PN, :], scalar=rstd[0:PN, 0:1],
                                                   in1=vec[0:PN, 2, :], op0=ALU.mult, op1=ALU.add).then_inc(s_ha, 1)
                    if c == C_HA and L == 1:
                        v.wait_ge(s_h, n + 1)
                        v.tensor_tensor(ha[0:PN, :], psH[0:PN, k, :], vec[0:PN, 5, :], ALU.add).then_inc(s_ha, 1)
                    if c == C_U:
                        v.wait_ge(s_ha, n + 1)
                        wait(v, s_x1, n)
                        if L == 1:
                            v.wait_ge(s_xr2, n + 1 - T)
                        v.scalar_tensor_tensor(out=u[0:PN, :], in0=ha[0:PN, :], scalar=0.0,
                                               in1=xs[0:PN, k, :] if L == 0 else xr2[0:PN, k, :],
                                               op0=ALU.max, op1=ALU.add, accum_out=total[0:PN, 1:2]).then_inc(s_u, 1)
                        minus_mean(n, 1, s_u)
                    if c == C_HS and L == 0:
                        v.wait_ge(s_nmean[1], n + 1)
                        v.scalar_tensor_tensor(out=hs[0:PN, :], in0=u[0:PN, :], scalar=nmean[0:PN, 1:2],
                                               in1=vec[0:PN, 3, :], op0=ALU.add, op1=ALU.mult).then_inc(s_hs, 1)
                    if c == C_RSTD1:
                        wait(v, s_x1, n)
                        inverse(n, 1)
                    if c == C_SHIFT:
                        v.wait_ge(s_rstd[1], n + 1)
                        v.tensor_tensor(shift[0:PN, :], nmean[0:PN, 1:2], rstd[0:PN, 1:2], ALU.mult).then_inc(s_shift, 1)
                        if L == 0:
                            wait(v, s_sd1, n)
                            v.tensor_scalar(var1[0:PN, :], spread[0:PN, 1:2], rstd[0:PN, 1:2], rstd[0:PN, 1:2],
                                            ALU.mult, ALU.mult).then_inc(s_var1, 1)
                    if c == C_RSTD and L == 0:
                        v.wait_ge(s_sd1, n + 1)
                        v.reciprocal(rstd1[0:PN, :], sd1[0:PN, :]).then_inc(s_rstd1, 1)
                    if c == C_H1 and L == 0:
                        v.wait_ge(s_rstd1, n + 1)
                        v.tensor_tensor(scale1[0:PN, :], rstd1[0:PN, :], rstd[0:PN, 1:2], ALU.mult).then_inc(s_scale1, 1)
                        v.wait_ge(s_scale1, n + 1)
                        v.wait_ge(s_hs, n + 1)
                        wait(v, s_sth[k], 16 * j)
                        v.scalar_tensor_tensor(out=h1o[0:PN, k, :], in0=hs[0:PN, :], scalar=scale1[0:PN, :],
                                               in1=vec[0:PN, 4, :], op0=ALU.mult, op1=ALU.add).then_inc(s_h1, 1)

                def period(t, k, j, jp, chunks, dense, norms):
                    if chunks:
                        keys(t, k, j)
                    for c in range(MAIN):
                        if chunks:
                            if c % GROUP == 0:
                                one_hots(t, k, c // GROUP)
                            if c in SPLIT:
                                split(t, k, c)
                        if dense:
                            dense_step(t - 1, 1 - k, c)
                        if norms and chunks:
                            norm_step(t - 2, k, j - 1, c)
                    for c in range(MAIN):
                        if norms and not chunks:
                            norm_step(t - 2, k, j - 1, c)

                over_periods(v, period)


def kernel(x, src, dst, L0_gnn_w_self, L0_gnn_w_neigh, L0_gnn_bias, L0_gnn_gamma, L0_gnn_beta,
           L1_gnn_W_l, L1_gnn_b_l, L1_gnn_W_r, L1_gnn_gamma, L1_gnn_beta):
    import numpy as np
    import concourse.bacc as bacc
    from concourse.bass_utils import run_bass_kernel_spmd

    w = np.stack([np.asarray(a) for a in (L0_gnn_w_self, L0_gnn_w_neigh, L1_gnn_W_r, L1_gnn_W_l)])
    w = w.reshape(2, 2, D, KC, 128).transpose(4, 0, 1, 3, 2)
    vecs = np.stack([np.asarray(a) for a in (L0_gnn_bias, L0_gnn_gamma, L0_gnn_beta, L1_gnn_gamma, L1_gnn_beta,
                                             L1_gnn_b_l)])
    arrays = {
        "x": np.ascontiguousarray(x), "src": np.ascontiguousarray(src), "dst": np.ascontiguousarray(dst),
        "wT": np.ascontiguousarray(w.reshape(128, 4 * KC * D)),
        "vecs": np.ascontiguousarray(np.broadcast_to(vecs.reshape(1, 6 * D), (128, 6 * D))),
        "consts": constants(np),
    }
    nc = bacc.Bacc("TRN2", target_bir_lowering=False, num_devices=1)
    ins = [nc.dram_tensor(n, a.shape, mybir.dt.from_np(a.dtype), kind="ExternalInput").ap() for n, a in arrays.items()]
    out = nc.dram_tensor("out", (N, D), F32, kind="ExternalOutput").ap()
    h1 = nc.dram_tensor("h1", (N, D), F32, kind="Internal").ap()
    x1 = nc.dram_tensor("x1", (N, D), F32, kind="Internal").ap()
    sums = nc.dram_tensor("sums", (N + PN, DX), F32, kind="Internal").ap()
    build(nc, *ins, out, h1, x1, sums)
    r = run_bass_kernel_spmd(nc, [arrays], core_ids=[0])
    return r.results[0]["out"]
```
